# Optimizing a Trainium2 kernel written in Bass

```python
import numpy as np
import jax
import jax.numpy as jnp

def _softmax(x, axis=-1):
    return jax.nn.softmax(x, axis=axis)

def _gelu(x):
    return jax.nn.gelu(x, approximate=True)

def _silu(x):
    return jax.nn.silu(x)

def _sigmoid(x):
    return jax.nn.sigmoid(x)

def _layernorm(x, axis=-1, eps=1e-05):
    m = jnp.mean(x, axis=axis, keepdims=True)
    v = jnp.var(x, axis=axis, keepdims=True)
    return (x - m) / jnp.sqrt(v + eps)

def _scatter_add(tgt, idx, src, axis=0):
    return tgt.at[idx].add(src)

def _segment_sum(src, seg, n):
    return jax.ops.segment_sum(src, seg, n)
kernel_name = 'mk_perceiver_d1_seqx_r2_104438'

def setup_inputs(seed: int=0):
    np.random.seed(seed)
    _w = jnp.asarray

    def _rec_inputs():
        import jax
        import jax.numpy as jnp
        _rk = jax.random.key(seed)
        x = -0.0003929 + 0.9999 * jax.random.normal(jax.random.fold_in(_rk, 1), (16, 64, 512), jnp.float32)
        _lenS = 64 - jax.random.randint(jax.random.fold_in(_rk, 7), (16,), 0, max(1, 64 // 4) + 1, jnp.int32)
        _lenS2 = 1601 - jax.random.randint(jax.random.fold_in(_rk, 8), (16,), 0, max(1, 1601 // 4) + 1, jnp.int32)
        _ctx_1024P = jax.random.normal(jax.random.fold_in(_rk, 11), (16, 16, 512), jnp.float32)
        _ctx_1024c = jax.random.dirichlet(jax.random.fold_in(_rk, 511), 0.3 * jnp.ones((16,), jnp.float32), (16, 1601))
        _ctx_1024t = jnp.einsum('bsk,bkd->bsd', _ctx_1024c, _ctx_1024P)
        _ctx_1024t = _ctx_1024t * jax.lax.rsqrt(jnp.mean(jnp.square(_ctx_1024t)) + 1e-12) * 0.953939
        ctx_1024 = 2.81802e-05 + 1.00001 * (_ctx_1024t + 0.3 * jax.random.normal(jax.random.fold_in(_rk, 611), (16, 1601, 512), jnp.float32))
        return (x, ctx_1024)
    x, ctx_1024 = _rec_inputs()

    def _L0_xattn_setup():
        import jax, jax.numpy as jnp
        import numpy as np
        E = 512
        NUM_HEADS = 16
        DK = E // NUM_HEADS
        EPS = 1e-05
        NEG_INF = -jnp.inf

        def layer_norm(x, g, b):
            mu = jnp.mean(x, axis=-1, keepdims=True)
            var = jnp.var(x, axis=-1, keepdims=True)
            return (x - mu) * jax.lax.rsqrt(var + EPS) * g + b

        def self_attn(x, Wq, Wk, Wv):
            Q, K, V = (x @ Wq, x @ Wk, x @ Wv)
            energy = jnp.einsum('bqd,bkd->bqk', Q, K)
            S = energy.shape[-1]
            lengths = jnp.sum(energy[:, 0] != 0, axis=-1)
            kidx = jnp.arange(S)
            pad = kidx[None, None, :] >= lengths[:, None, None]
            causal = kidx[None, :] < kidx[:, None]
            causal = (kidx[None, :] > kidx[:, None])[None]
            energy = jnp.where(pad | causal, NEG_INF, energy)
            score = jax.nn.softmax(energy / np.sqrt(DK), axis=-1)
            return jnp.einsum('bqk,bkd->bqd', score, V)

        def cross_attn(x, context, Wq, Wk, Wv):
            Q = x @ Wq
            K, V = (context @ Wk, context @ Wv)
            energy = jnp.einsum('bqd,bkd->bqk', Q, K)
            Sk = energy.shape[-1]
            lengths = jnp.sum(energy[:, 0] != 0, axis=-1)
            kidx = jnp.arange(Sk)
            pad = kidx[None, None, :] >= lengths[:, None, None]
            energy = jnp.where(pad, NEG_INF, energy)
            score = jax.nn.softmax(energy / np.sqrt(DK), axis=-1)
            return jnp.einsum('bqk,bkd->bqd', score, V)
        key = jax.random.key(seed)
        ks = jax.random.split(key, 12)
        B, S = (8, 1024)
        s = 1.0 / np.sqrt(E)
        inp = {'x': jax.random.normal(ks[0], (B, S, E), jnp.float32), 'context': jax.random.normal(ks[1], (B, S, E), jnp.float32), 'Wq1': jax.random.normal(ks[2], (E, E), jnp.float32) * s, 'Wk1': jax.random.normal(ks[3], (E, E), jnp.float32) * s, 'Wv1': jax.random.normal(ks[4], (E, E), jnp.float32) * s, 'Wq2': jax.random.normal(ks[5], (E, E), jnp.float32) * s, 'Wk2': jax.random.normal(ks[6], (E, E), jnp.float32) * s, 'Wv2': jax.random.normal(ks[7], (E, E), jnp.float32) * s, 'fc1_w': jax.random.normal(ks[8], (E, E), jnp.float32) * s, 'fc1_b': jnp.zeros((E,), jnp.float32), 'fc2_w': jax.random.normal(ks[9], (E, E), jnp.float32) * s, 'fc2_b': jnp.zeros((E,), jnp.float32), 'ln1_g': jnp.ones((E,), jnp.float32), 'ln1_b': jnp.zeros((E,), jnp.float32), 'ln2_g': jnp.ones((E,), jnp.float32), 'ln2_b': jnp.zeros((E,), jnp.float32), 'ln3_g': jnp.ones((E,), jnp.float32), 'ln3_b': jnp.zeros((E,), jnp.float32)}
        return inp
    _L0_xattn_all = _L0_xattn_setup()
    _L0_xattn_in = {k: v for k, v in _L0_xattn_all.items() if k in ('Wq1', 'Wk1', 'Wv1', 'Wq2', 'Wk2', 'Wv2', 'fc1_w', 'fc1_b', 'fc2_w', 'fc2_b', 'ln1_g', 'ln1_b', 'ln2_g', 'ln2_b', 'ln3_g', 'ln3_b')}
    del _L0_xattn_all

    def _L0_attn_setup():
        import jax, jax.numpy as jnp
        import numpy as np
        DIM = 512
        HIDDEN = 768
        K = 4
        ALPHA_LOG_SCALE = -8.0

        def _causal_depthwise_conv(x, w, b):
            T = x.shape[1]
            xp = jnp.pad(x, ((0, 0), (K - 1, 0), (0, 0)))
            y = b
            for k in range(K):
                y = y + w[:, k] * xp[:, k:k + T, :]
            return y

        def _rglru_scan(alpha, xs):

            def combine(c1, c2):
                a1, x1 = c1
                a2, x2 = c2
                return (a1 * a2, a2 * x1 + x2)
            _, h = jax.lax.associative_scan(combine, (alpha, xs), axis=1)
            return h
        key = jax.random.key(seed)
        ks = jax.random.split(key, 7)
        x = jax.random.normal(ks[0], (8, 1024, DIM), dtype=jnp.float32)
        W_in = jax.random.normal(ks[1], (2 * HIDDEN, DIM), dtype=jnp.float32) * DIM ** (-0.5)
        conv_w = jax.random.normal(ks[2], (HIDDEN, K), dtype=jnp.float32) * (1.0 / K) ** 0.5
        conv_b = jax.random.normal(ks[3], (HIDDEN,), dtype=jnp.float32) * 0.02
        W_gates = jax.random.normal(ks[4], (2 * HIDDEN, HIDDEN), dtype=jnp.float32) * HIDDEN ** (-0.5)
        b_gates = jnp.zeros((2 * HIDDEN,), dtype=jnp.float32)
        forget_base = jnp.linspace(-4.323, -9.0, HIDDEN, dtype=jnp.float32)
        W_out = jax.random.normal(ks[5], (DIM, HIDDEN), dtype=jnp.float32) * HIDDEN ** (-0.5)
        return {'x': x, 'W_in': W_in, 'conv_w': conv_w, 'conv_b': conv_b, 'W_gates': W_gates, 'b_gates': b_gates, 'forget_base': forget_base, 'W_out': W_out}
    _L0_attn_all = _L0_attn_setup()
    _L0_attn_in = {k: v for k, v in _L0_attn_all.items() if k in ('W_in', 'conv_w', 'conv_b', 'W_gates', 'b_gates', 'forget_base', 'W_out')}
    del _L0_attn_all

    def _L0_ffn_setup():
        import jax, jax.numpy as jnp
        import numpy as np
        NUM_EXPERTS = 8
        TOP_K = 2
        CAPACITY_FACTOR = 1.25
        key = jax.random.key(seed)
        ks = jax.random.split(key, 5)
        B, S, D, H, E = (4, 1024, 512, 1024, NUM_EXPERTS)
        scale = 0.02
        return {'x': jax.random.normal(ks[0], (B, S, D), dtype=jnp.float32), 'gate_w': jax.random.normal(ks[1], (E, D), dtype=jnp.float32) * scale, 'gate_proj_w': jax.random.normal(ks[2], (E, H, D), dtype=jnp.float32) * scale, 'up_proj_w': jax.random.normal(ks[3], (E, H, D), dtype=jnp.float32) * scale, 'down_proj_w': jax.random.normal(ks[4], (E, D, H), dtype=jnp.float32) * scale}
    _L0_ffn_all = _L0_ffn_setup()
    _L0_ffn_in = {k: v for k, v in _L0_ffn_all.items() if k in ('gate_w', 'gate_proj_w', 'up_proj_w', 'down_proj_w')}
    del _L0_ffn_all
    return {'x': x, 'ctx_1024': ctx_1024, 'L0_xattn_Wq1': _L0_xattn_in['Wq1'], 'L0_xattn_Wk1': _L0_xattn_in['Wk1'], 'L0_xattn_Wv1': _L0_xattn_in['Wv1'], 'L0_xattn_Wq2': _L0_xattn_in['Wq2'], 'L0_xattn_Wk2': _L0_xattn_in['Wk2'], 'L0_xattn_Wv2': _L0_xattn_in['Wv2'], 'L0_xattn_fc1_w': _L0_xattn_in['fc1_w'], 'L0_xattn_fc1_b': _L0_xattn_in['fc1_b'], 'L0_xattn_fc2_w': _L0_xattn_in['fc2_w'], 'L0_xattn_fc2_b': _L0_xattn_in['fc2_b'], 'L0_xattn_ln1_g': _L0_xattn_in['ln1_g'], 'L0_xattn_ln1_b': _L0_xattn_in['ln1_b'], 'L0_xattn_ln2_g': _L0_xattn_in['ln2_g'], 'L0_xattn_ln2_b': _L0_xattn_in['ln2_b'], 'L0_xattn_ln3_g': _L0_xattn_in['ln3_g'], 'L0_xattn_ln3_b': _L0_xattn_in['ln3_b'], 'L0_attn_W_in': _L0_attn_in['W_in'], 'L0_attn_conv_w': _L0_attn_in['conv_w'], 'L0_attn_conv_b': _L0_attn_in['conv_b'], 'L0_attn_W_gates': _L0_attn_in['W_gates'], 'L0_attn_b_gates': _L0_attn_in['b_gates'], 'L0_attn_forget_base': _L0_attn_in['forget_base'], 'L0_attn_W_out': _L0_attn_in['W_out'], 'L0_ffn_gate_w': _L0_ffn_in['gate_w'], 'L0_ffn_gate_proj_w': _L0_ffn_in['gate_proj_w'], 'L0_ffn_up_proj_w': _L0_ffn_in['up_proj_w'], 'L0_ffn_down_proj_w': _L0_ffn_in['down_proj_w']}

def reference(x, ctx_1024, L0_xattn_Wq1, L0_xattn_Wk1, L0_xattn_Wv1, L0_xattn_Wq2, L0_xattn_Wk2, L0_xattn_Wv2, L0_xattn_fc1_w, L0_xattn_fc1_b, L0_xattn_fc2_w, L0_xattn_fc2_b, L0_xattn_ln1_g, L0_xattn_ln1_b, L0_xattn_ln2_g, L0_xattn_ln2_b, L0_xattn_ln3_g, L0_xattn_ln3_b, L0_attn_W_in, L0_attn_conv_w, L0_attn_conv_b, L0_attn_W_gates, L0_attn_b_gates, L0_attn_forget_base, L0_attn_W_out, L0_ffn_gate_w, L0_ffn_gate_proj_w, L0_ffn_up_proj_w, L0_ffn_down_proj_w):
    import jax
    import jax.numpy as jnp

    def _L0_xattn_ref(x, context, Wq1, Wk1, Wv1, Wq2, Wk2, Wv2, fc1_w, fc1_b, fc2_w, fc2_b, ln1_g, ln1_b, ln2_g, ln2_b, ln3_g, ln3_b):
        import jax, jax.numpy as jnp
        import numpy as np
        E = 512
        NUM_HEADS = 16
        DK = E // NUM_HEADS
        EPS = 1e-05
        NEG_INF = -jnp.inf

        def layer_norm(x, g, b):
            mu = jnp.mean(x, axis=-1, keepdims=True)
            var = jnp.var(x, axis=-1, keepdims=True)
            return (x - mu) * jax.lax.rsqrt(var + EPS) * g + b

        def self_attn(x, Wq, Wk, Wv):
            Q, K, V = (x @ Wq, x @ Wk, x @ Wv)
            energy = jnp.einsum('bqd,bkd->bqk', Q, K)
            S = energy.shape[-1]
            lengths = jnp.sum(energy[:, 0] != 0, axis=-1)
            kidx = jnp.arange(S)
            pad = kidx[None, None, :] >= lengths[:, None, None]
            causal = kidx[None, :] < kidx[:, None]
            causal = (kidx[None, :] > kidx[:, None])[None]
            energy = jnp.where(pad | causal, NEG_INF, energy)
            score = jax.nn.softmax(energy / np.sqrt(DK), axis=-1)
            return jnp.einsum('bqk,bkd->bqd', score, V)

        def cross_attn(x, context, Wq, Wk, Wv):
            Q = x @ Wq
            K, V = (context @ Wk, context @ Wv)
            energy = jnp.einsum('bqd,bkd->bqk', Q, K)
            Sk = energy.shape[-1]
            lengths = jnp.sum(energy[:, 0] != 0, axis=-1)
            kidx = jnp.arange(Sk)
            pad = kidx[None, None, :] >= lengths[:, None, None]
            energy = jnp.where(pad, NEG_INF, energy)
            score = jax.nn.softmax(energy / np.sqrt(DK), axis=-1)
            return jnp.einsum('bqk,bkd->bqd', score, V)
        z = self_attn(x, Wq1, Wk1, Wv1)
        x = layer_norm(x + z, ln1_g, ln1_b)
        z = cross_attn(x, context, Wq2, Wk2, Wv2)
        x = layer_norm(x + z, ln2_g, ln2_b)
        z = jax.nn.relu(x @ fc1_w + fc1_b)
        z = z @ fc2_w + fc2_b
        return layer_norm(x + z, ln3_g, ln3_b)

    def _L0_attn_ref(x, W_in, conv_w, conv_b, W_gates, b_gates, forget_base, W_out):
        import jax, jax.numpy as jnp
        import numpy as np
        DIM = 512
        HIDDEN = 768
        K = 4
        ALPHA_LOG_SCALE = -8.0

        def _causal_depthwise_conv(x, w, b):
            T = x.shape[1]
            xp = jnp.pad(x, ((0, 0), (K - 1, 0), (0, 0)))
            y = b
            for k in range(K):
                y = y + w[:, k] * xp[:, k:k + T, :]
            return y

        def _rglru_scan(alpha, xs):

            def combine(c1, c2):
                a1, x1 = c1
                a2, x2 = c2
                return (a1 * a2, a2 * x1 + x2)
            _, h = jax.lax.associative_scan(combine, (alpha, xs), axis=1)
            return h
        u = jnp.einsum('ntc,hc->nth', x, W_in)
        gate, xh = jnp.split(u, 2, axis=-1)
        xh = _causal_depthwise_conv(xh, conv_w, conv_b)
        g = jnp.einsum('nth,gh->ntg', xh, W_gates) + b_gates
        forget, inp = jnp.split(g, 2, axis=-1)
        log_alpha = ALPHA_LOG_SCALE * jax.nn.softplus(forget_base) * jax.nn.sigmoid(forget)
        alpha = jnp.exp(log_alpha)
        beta = jnp.sqrt(1.0 - alpha ** 2 + 1e-06)
        xs = beta * jax.nn.sigmoid(inp) * xh
        h = _rglru_scan(alpha, xs)
        out = jnp.einsum('nth,dh->ntd', jax.nn.gelu(gate, approximate=False) * h, W_out)
        return out

    def _L0_ffn_ref(x, gate_w, gate_proj_w, up_proj_w, down_proj_w):
        import jax, jax.numpy as jnp
        import numpy as np
        NUM_EXPERTS = 8
        TOP_K = 2
        CAPACITY_FACTOR = 1.25
        B, S, D = x.shape
        E, K = (NUM_EXPERTS, TOP_K)
        T = B * S
        xf = x.reshape(T, D)
        logits = xf @ gate_w.T
        probs = jax.nn.softmax(logits, axis=-1)
        top_p, top_i = jax.lax.top_k(probs, K)
        w = top_p / (jnp.sum(top_p, axis=-1, keepdims=True) + 1e-09)
        capacity = int(CAPACITY_FACTOR * T / E)
        oh = jax.nn.one_hot(top_i, E, dtype=jnp.int32)
        rank = jnp.cumsum(oh, axis=0) - 1
        my_rank = jnp.sum(rank * oh, axis=-1)
        keep = (my_rank < capacity).astype(w.dtype)
        comb = jnp.einsum('tk,tke->te', w * keep, oh.astype(w.dtype))
        out = jnp.zeros_like(xf)
        for e in range(E):
            g = jax.nn.silu(xf @ gate_proj_w[e].T)
            u = xf @ up_proj_w[e].T
            y = g * u @ down_proj_w[e].T
            out = out + comb[:, e:e + 1] * y
        return out.reshape(B, S, D)
    x = x + _L0_xattn_ref(_layernorm(x, axis=-1), ctx_1024, L0_xattn_Wq1, L0_xattn_Wk1, L0_xattn_Wv1, L0_xattn_Wq2, L0_xattn_Wk2, L0_xattn_Wv2, L0_xattn_fc1_w, L0_xattn_fc1_b, L0_xattn_fc2_w, L0_xattn_fc2_b, L0_xattn_ln1_g, L0_xattn_ln1_b, L0_xattn_ln2_g, L0_xattn_ln2_b, L0_xattn_ln3_g, L0_xattn_ln3_b)
    x = x + _L0_attn_ref(_layernorm(x, axis=-1), L0_attn_W_in, L0_attn_conv_w, L0_attn_conv_b, L0_attn_W_gates, L0_attn_b_gates, L0_attn_forget_base, L0_attn_W_out)
    x = x + _L0_ffn_ref(_layernorm(x, axis=-1), L0_ffn_gate_w, L0_ffn_gate_proj_w, L0_ffn_up_proj_w, L0_ffn_down_proj_w)
    return x

_drawn_inputs = setup_inputs


def setup_inputs(seed=0):
    import zlib

    import numpy as np

    out = dict(_drawn_inputs(seed))
    spreads = {'L0_xattn_fc1_b': (0.0, 0.1),
     'L0_xattn_fc2_b': (0.0, 0.1),
     'L0_xattn_ln1_g': (1.0, 0.2),
     'L0_xattn_ln1_b': (0.0, 0.1),
     'L0_xattn_ln2_g': (1.0, 0.2),
     'L0_xattn_ln2_b': (0.0, 0.1),
     'L0_xattn_ln3_g': (1.0, 0.2),
     'L0_xattn_ln3_b': (0.0, 0.1),
     'L0_attn_b_gates': (0.0, 0.653)}
    factors = {'L0_attn_conv_b': 3.258}
    for name, (base, spread) in spreads.items():
        noise = np.random.default_rng([zlib.crc32(name.encode()), seed]).standard_normal(out[name].shape)
        drawn = base * np.exp(spread * noise) if base else spread * noise
        out[name] = jnp.asarray(drawn.astype(out[name].dtype))
    for name, factor in factors.items():
        out[name] = (out[name] * factor).astype(out[name].dtype)
    return out
```

```python
from contextlib import ExitStack

import concourse.bass as bass
from concourse import mybir
from concourse.alu_op_type import AluOpType as ALU

ACT = mybir.ActivationFunctionType
AX_X = mybir.AxisListType.X
F32 = mybir.dt.float32
U32 = mybir.dt.uint32
I16 = mybir.dt.int16

P = 128
B, S, D = 16, 64, 512
T = B * S
NT = T // P
DC = D // P
SK = 1601
KT = SK // P
TAIL = SK - KT * P
KB = KT // 4
HID = 768
HC = HID // P
NE, TOPK, FF = 8, 2, 1024
FC = FF // P
CAP = int(1.25 * T / NE)
SLOTS = TOPK * CAP
NS = -(-SLOTS // P)
LAST = SLOTS - (NS - 1) * P
TRASH = NE * SLOTS
EPS = 1e-5
SCALE = float((D // 16) ** -0.5)
NEG = -1e38
CB = 3
ATANH_TERMS = 9


def dense_groups():
    g = [("m1", c) for c in range(DC)]
    g += [("t0", i) for i in range(NT)]
    g += [("gt", c, h) for h in range(2) for c in range(DC)]
    g += [("e", h) for h in range(2)]
    g += [("v", i) for i in range(NT)]
    g += [("len", h) for h in range(2)]
    g += [("m2", c) for c in range(DC)]
    g += [("pt", i) for i in range(NT)]
    g += [("z", i) for i in range(NT)]
    g += [("t1", i) for i in range(NT)]
    g += [("q", c, h) for h in range(2) for c in range(DC)]
    g += [("z2", i) for i in range(NT)]
    g += [("t2", i) for i in range(NT)]
    g += [("f1", c, h) for h in range(2) for c in range(DC)]
    g += [("f2", i) for i in range(NT)]
    g += [("t4", i) for i in range(NT)]
    g += [("xh", c, h) for c in range(HC) for h in range(2)]
    g += [("ga", c, h) for c in range(HC) for h in range(2)]
    g += [("fg", c, h) for c in range(HC) for h in range(2)]
    g += [("ig", c, h) for h in range(2) for c in range(HC)]
    g += [("wo", i) for i in range(NT)]
    g += [("t5", i) for i in range(NT)]
    g += [("lg",), ("rk",)]
    return g


def perceiver_program(nc, a, out):
    with ExitStack() as ctx:
        def sb(name, shape, dt=F32):
            return ctx.enter_context(nc.sbuf_tensor(name, shape, dt))

        def sem(name):
            return ctx.enter_context(nc.semaphore(name))

        ps = ctx.enter_context(nc.psum_tensor("ps", [P, 8, 512], F32))
        group_at = {name: (g % 8, g // 8) for g, name in enumerate(dense_groups())}
        filled = [sem(f"filled{k}") for k in range(8)]
        evacuated = [sem(f"evacuated{k}") for k in range(8)]

        def bank(*g):
            return ps[:, group_at[g][0], :]

        def wait_bank_free(pe, *g):
            k, use = group_at[g]
            if use:
                pe.wait_ge(evacuated[k], use)

        def wait_filled(eng, *g):
            eng.wait_ge(filled[group_at[g][0]], group_at[g][1] + 1)

        def wait_evacuated(eng, *g):
            eng.wait_ge(evacuated[group_at[g][0]], group_at[g][1] + 1)

        def signals_filled(ins, *g):
            ins.then_inc(filled[group_at[g][0]], 1)

        def signals_evacuated(ins, *g):
            ins.then_inc(evacuated[group_at[g][0]], 1)

        xr = sb("xr", [P, NT, D])
        hr = sb("hr", [P, NT, D])
        hT = sb("hT", [P, DC, T])
        ident = sb("ident", [P, P])
        own = sb("own", [P, P])
        cmask = sb("cmask", [P, P])
        kidx_self = sb("kidx_self", [P, P])
        sel = sb("sel", [P, P])
        tri = sb("tri", [P, P])
        ones = sb("ones", [P, P])
        lnw = sb("lnw", [P, 7, D])
        stats = sb("stats", [P, NT, 6])
        mv = sb("mv", [P, NT, 2])
        veps = sb("veps", [P, NT])
        rstd = sb("rstd", [P, NT])
        consts = sb("consts", [P, 2])
        cnt = sb("cnt", [P, NT])
        lens = sb("lens", [P, NT])
        rlen = sb("rlen", [P, NT])
        onel = sb("onel", [P, NT])
        mx = sb("mx", [P, NT])
        rsum = sb("rsum", [P, NT])
        rinv = sb("rinv", [P, NT])
        fc1b = sb("fc1b", [P, DC])
        convw = sb("convw", [P, HC, 4])
        convb = sb("convb", [P, HC])
        bgate = sb("bgate", [P, 2 * HC])
        fbase = sb("fbase", [P, HC])
        lac = sb("lac", [P, 8, HC])
        gwT = sb("gwT", [P, DC, NE])
        slot_at = sb("slot_at", [P, 2, NT * TOPK])
        eidx = sb("eidx", [P, NT * TOPK, NE])
        lg = sb("lg", [P, NT, NE])
        top8 = sb("top8", [P, NT, 8])
        topi = sb("topi", [P, NT, 8], U32)
        oh = sb("oh", [P, NT * TOPK, NE])
        rk = sb("rk", [P, NT * TOPK, NE])
        rt = sb("rt", [P, 8, NT * TOPK])
        scat = sb("scat", [P, NT * TOPK], U32)
        gath = sb("gath", [P, NT * TOPK], U32)
        s_cnt = sb("s_cnt", [S, CB, 8])
        BIG = 34920
        big = sb("big", [P, BIG])

        def at(off, *shape):
            n = 1
            for x in shape:
                n *= x
            assert off + n <= BIG, (off, shape)
            v = big[:, off:off + n]
            if len(shape) == 2:
                v = v.rearrange("p (a b) -> p a b", b=shape[1])
            return v

        wq1T, wk1T, m1 = at(6656, DC, D), at(8704, DC, D), at(10752, DC, D)
        wq2T, wk2T, gT = at(12800, DC, D), at(14848, DC, D), at(16896, DC, T)
        wv1, sP, m2, vv = at(20992, DC, D), at(23040, NT, P), at(24064, DC, D), at(26112, NT, D)
        ne, pad, sT = at(6656, NT, P), at(7680, NT, P), at(16896, NT, P)
        zeros = at(33316, D)
        CW = (KT + 1) * D
        cbuf = [at(j * CW, KT + 1, D) for j in range(CB)]
        cT = [hT[:, :, 0:512], hT[:, :, 512:1024]]
        qT = at(19968, DC, T)
        es = [at(24064 + j * SK, SK) for j in range(CB)]
        pts = at(28867, KT + 1, S)
        qs = [at(29699 + j * 256, DC, S) for j in range(CB)]
        kidx, wv2, kpad = at(30467, 801).bitcast(I16), at(31268, DC, D), at(33316, SK)
        fc1, fc2, f1T = at(6656, DC, D), at(8704, DC, D), at(24064, DC, T)
        wga, win, alp = at(0, HC, 2 * HID), at(13312, DC, 2 * HID), at(13312, HC, T)
        xhc, gel = at(19456, HC, T), at(25600, HC, T)
        bet = [at(9216 + c * T, T) if c < 4 else at(31744 + (c - 4) * T, T) for c in range(HC)]
        wout = hT[:].rearrange("p c t -> p (c t)")[:, 0:HC * D].rearrange("p (c d) -> p c d", d=D)
        hflat = hr[:].rearrange("p i d -> p (i d)")
        raw = [hflat[:, j * T:(j + 1) * T] for j in range(2)]
        sgi = [hflat[:, 2 * T + j * 512:2 * T + (j + 1) * 512] for j in range(2)]
        EW = 2 * DC * FF + FC * D
        wg = [at(j * EW, DC, FF) for j in range(2)]
        wu = [at(j * EW + DC * FF, DC, FF) for j in range(2)]
        wd = [at(j * EW + 2 * DC * FF, FC, D) for j in range(2)]
        hid = [at(2 * EW + j * FC * SLOTS, FC, SLOTS) for j in range(2)]
        ye = [at(29696 + j * NS * D, NS, D) for j in range(2)]
        yg = [at(32768 + j * 2 * D, TOPK, D) for j in range(2)]
        xe = [hflat[:, j * NS * D:(j + 1) * NS * D].rearrange("p (s d) -> p s d", d=D) for j in range(2)]
        htf = hT[:].rearrange("p c t -> p (c t)")
        xeT = [htf[:, j * DC * SLOTS:(j + 1) * DC * SLOTS].rearrange("p (c s) -> p c s", s=SLOTS)
               for j in range(2)]
        sg = [htf[:, 2560 + j * SLOTS:2560 + (j + 1) * SLOTS] for j in range(2)]

        xs = nc.dram_tensor("xs", (TRASH + TOPK * T, D), F32, kind="Internal").ap()
        ys = nc.dram_tensor("ys", (TRASH, D), F32, kind="Internal").ap()

        x_in = [sem(f"x_in{j}") for j in range(4)]
        consts_in, lnw_in, wq1_in, wq2_in, wv1_in = map(sem, ("consts_in", "lnw_in", "wq1_in", "wq2_in", "wv1_in"))
        wv2_in, fc_in, win_in, wga_in, wout_in = map(sem, ("wv2_in", "fc_in", "win_in", "wga_in", "wout_in"))
        zero_set, xs_zeroed, consts_set = sem("zero_set"), sem("xs_zeroed"), sem("consts_set")
        ln_stats, ln_mv, ln_veps, ln_rstd, ln_norm, ln_gain, ln_out = map(
            sem, ("ln_stats", "ln_mv", "ln_veps", "ln_rstd", "ln_norm", "ln_gain", "ln_out"))
        res_sum, res_half = sem("res_sum"), sem("res_half")
        sa_step, sa_cnt, sa_shift, sa_exp, sa_prob = map(sem, ("sa_step", "sa_cnt", "sa_shift", "sa_exp", "sa_prob"))
        ctx_in = [sem(f"ctx_in{j}") for j in range(CB)]
        q_ready, tp_done, tp_act, tp_dve, e_done, e_evac = map(
            sem, ("q_ready", "tp_done", "tp_act", "tp_dve", "e_done", "e_evac"))
        cnt_ne, cnt_done, len_done, sm_step, exp_done = map(sem, ("cnt_ne", "cnt_done", "len_done", "sm_step", "exp_done"))
        pt_done, pt_evac, o_done, o_evac = map(sem, ("pt_done", "pt_evac", "o_done", "o_evac"))
        conv_step, conv_done, lac_step, lac_done = map(sem, ("conv_step", "conv_done", "lac_step", "lac_done"))
        alpha_done, square_done, alpha_reset, beta_done = map(sem, ("alpha_done", "square_done", "alpha_reset", "beta_done"))
        rec_step, gated = sem("rec_step"), sem("gated")
        rt_shift, rt_exp, rt_step, oh_done, idx_done = map(sem, ("rt_shift", "rt_exp", "rt_step", "oh_done", "idx_done"))
        scattered = sem("scattered")
        wgu_in, wd_in = [sem(f"wgu_in{j}") for j in range(2)], [sem(f"wd_in{j}") for j in range(2)]
        xe_in = [sem(f"xe_in{j}") for j in range(2)]
        xt_done, xt_evac, gu_done, silu_done, hid_done, y_done, y_evac = map(
            sem, ("xt_done", "xt_evac", "gu_done", "silu_done", "hid_done", "y_done", "y_evac"))
        y_out = [sem(f"y_out{j}") for j in range(2)]
        y_all = sem("y_all")
        yg_in = [sem(f"yg_in{j}") for j in range(2)]
        mix_step, out_ready, out_done = map(sem, ("mix_step", "out_ready", "out_done"))

        LAC_STEPS = 2 + 3 + 2 + 2 * (ATANH_TERMS - 2) + 4

        block = ctx.enter_context(nc.Block())

        @block.sync
        def _(sp):
            def load(dst, src, signal):
                sp.dma_start(dst, src).then_inc(signal, 16)

            def weights(dst, src, signal):
                load(dst, src.rearrange("(c p) n -> p c n", p=P), signal)

            x_rows = a["x"].rearrange("(i p) d -> p i d", p=P)
            load(xr[:, 0:2, :], x_rows[:, 0:2, :], x_in[0])
            weights(wq1T, a["wq1T"], wq1_in)
            weights(wk1T, a["wk1T"], wq1_in)
            for j in range(1, 4):
                load(xr[:, 2 * j:2 * j + 2, :], x_rows[:, 2 * j:2 * j + 2, :], x_in[j])
            for t, name in ((ident, "ident"), (own, "own"), (cmask, "cmask"), (kidx_self, "kidx_self"),
                            (sel, "sel"), (tri, "tri"), (ones, "ones"), (convw, "convw"), (fc1b, "fc1b"),
                            (convb, "convb"), (bgate, "bgate"), (fbase, "fbase"), (gwT, "gwT"),
                            (slot_at, "slot_at"), (eidx, "eidx")):
                load(t[:], a[name], consts_in)
            load(kidx[0:S, 0:SK], a["kidx"], consts_in)
            weights(wv1, a["wv1"], wv1_in)
            weights(wq2T, a["wq2T"], wq2_in)
            weights(wk2T, a["wk2T"], wq2_in)
            load(lnw[:], a["lnw"].partition_broadcast(P), lnw_in)
            weights(wv2, a["wv2"], wv2_in)

            def load_context(n, j):
                rows = a["ctx"][bass.ds(n, 1), :, :].rearrange("o k d -> (o k) d")
                load(cbuf[j][:, 0:KT, :], rows[0:KT * P, :].rearrange("(p k) d -> p k d", k=KT), ctx_in[j])
                load(cbuf[j][0:TAIL, KT, :], rows[KT * P:SK, :], ctx_in[j])

            load_context(0, 0)
            for h in range(2):
                for c in range(DC):
                    wait_evacuated(sp, "q", c, h)
            load_context(1, 1)
            load_context(2, 2)
            with sp.Fori(0, 4) as i:
                for j in range(CB):
                    sp.wait_ge(o_done, i * CB + (j + 1))
                    load_context(i * CB + (CB + j), j)
            sp.wait_ge(o_done, 13)
            load_context(15, 0)
            sp.wait_ge(o_done, 14)
            weights(fc1, a["fc1_w"], fc_in)
            weights(fc2, a["fc2_w"], fc_in)
            sp.wait_ge(o_done, 15)
            weights(win, a["w_inT"], win_in)
            for i in range(NT):
                wait_filled(sp, "f2", i)
            weights(wga, a["w_gatesT"], wga_in)
            for c in range(HC):
                for h in range(2):
                    wait_filled(sp, "ga", c, h)
            weights(wout, a["w_outT"], wout_in)

            def load_expert(n, j):
                one = a["w_gate"][bass.ds(n, 1), :, :].rearrange("o d f -> (o d) f")
                weights(wg[j], one, wgu_in[j])
                one = a["w_up"][bass.ds(n, 1), :, :].rearrange("o d f -> (o d) f")
                weights(wu[j], one, wgu_in[j])

            def load_down(n, j):
                one = a["w_down"][bass.ds(n, 1), :, :].rearrange("o f d -> (o f) d")
                weights(wd[j], one, wd_in[j])

            def load_rows(n, j):
                rows = xs[bass.ds(n * SLOTS, SLOTS), :]
                load(xe[j][:, 0:NS - 1, :], rows[0:(NS - 1) * P, :].rearrange("(s p) d -> p s d", p=P), xe_in[j])
                load(xe[j][0:LAST, NS - 1, :], rows[(NS - 1) * P:SLOTS, :], xe_in[j])

            for c in range(HC):
                for h in range(2):
                    wait_filled(sp, "ig", c, h)
            load_expert(0, 0)
            sp.wait_ge(gated, 2 * HC)
            load_down(0, 0)
            load_expert(1, 1)
            load_down(1, 1)
            sp.wait_ge(scattered, 16 * NT * TOPK)
            load_rows(0, 0)
            load_rows(1, 1)
            with sp.Fori(0, NE // 2 - 1) as i:
                for j in range(2):
                    sp.wait_ge(xt_done, NS * (i * 2 + (j + 1)))
                    load_rows(i * 2 + (2 + j), j)
                    sp.wait_ge(gu_done, 2 * FC * (i * 2 + (j + 1)))
                    load_expert(i * 2 + (2 + j), j)
                    sp.wait_ge(y_done, NS * (i * 2 + (j + 1)))
                    load_down(i * 2 + (2 + j), j)
            out_rows = out.rearrange("(i p) d -> p i d", p=P)
            for i in range(NT):
                sp.wait_ge(out_ready, i + 1)
                sp.dma_start(out_rows[:, i, :], xr[:, i, :]).then_inc(out_done, 16)
            sp.wait_ge(out_done, 16 * NT)

        @block.tensor
        def _(pe):
            def product(g, cols, pairs):
                wait_bank_free(pe, *g)
                for k, (lhsT, rhs) in enumerate(pairs):
                    mm = nc.tensor.matmul(bank(*g)[:, 0:cols], lhsT, rhs, start=(k == 0), stop=(k == len(pairs) - 1))
                signals_filled(mm, *g)

            def transpose_rows(g, rows):
                wait_bank_free(pe, *g)
                for c in range(DC):
                    mm = nc.tensor.transpose(bank(*g)[:, c * P:(c + 1) * P], rows[:, c * P:(c + 1) * P], ident[:])
                signals_filled(mm, *g)

            def tok(i):
                return slice(i * P, (i + 1) * P)

            def half(h):
                return slice(h * 512, (h + 1) * 512)

            pe.wait_ge(wq1_in, 32)
            for c in range(DC):
                product(("m1", c), 512, [(wq1T[:, e, tok(c)], wk1T[:, e, :]) for e in range(DC)])
            pe.wait_ge(consts_in, 16 * 16)
            for i in range(NT):
                pe.wait_ge(ln_norm, i + 1)
                transpose_rows(("t0", i), hr[:, i, :])
            for c in range(DC):
                wait_evacuated(pe, "m1", c)
            for h in range(2):
                for i in range(4 * h, 4 * h + 4):
                    wait_evacuated(pe, "t0", i)
                for c in range(DC):
                    product(("gt", c, h), 512, [(m1[:, d, tok(c)], hT[:, d, half(h)]) for d in range(DC)])
            for h in range(2):
                for c in range(DC):
                    wait_evacuated(pe, "gt", c, h)
                wait_bank_free(pe, "e", h)
                for q in range(4):
                    for d in range(DC):
                        mm = nc.tensor.matmul(bank("e", h)[:, q * P:(q + 1) * P], gT[:, d, tok(4 * h + q)],
                                              hT[:, d, tok(4 * h + q)], start=(d == 0), stop=(d == DC - 1))
                signals_filled(mm, "e", h)
            pe.wait_ge(wv1_in, 16)
            for i in range(NT):
                product(("v", i), 512, [(hT[:, d, tok(i)], wv1[:, d, :]) for d in range(DC)])
            for h in range(2):
                pe.wait_ge(sa_cnt, h + 1)
                product(("len", h), 4, [(sel[:], cnt[:, 4 * h:4 * h + 4])])
            pe.wait_ge(wq2_in, 32)
            for c in range(DC):
                product(("m2", c), 512, [(wq2T[:, e, tok(c)], wk2T[:, e, :]) for e in range(DC)])
            for i in range(NT):
                pe.wait_ge(sa_prob, i // 4 + 1)
                wait_bank_free(pe, "pt", i)
                signals_filled(nc.tensor.transpose(bank("pt", i)[:, 0:P], sP[:, i, :], ident[:]), "pt", i)
            for i in range(NT):
                wait_evacuated(pe, "pt", i)
                wait_evacuated(pe, "v", i)
                product(("z", i), 512, [(sT[:, i, :], vv[:, i, :])])
            for i in range(NT):
                pe.wait_ge(ln_out, i + 1)
                transpose_rows(("t1", i), hr[:, i, :])
            for c in range(DC):
                wait_evacuated(pe, "m2", c)
            for h in range(2):
                for i in range(4 * h, 4 * h + 4):
                    wait_evacuated(pe, "t1", i)
                for c in range(DC):
                    product(("q", c, h), 512, [(m2[:, d, tok(c)], hT[:, d, half(h)]) for d in range(DC)])
            for h in range(2):
                for c in range(DC):
                    wait_evacuated(pe, "q", c, h)

            def transpose_block(n, j, kb, first=False):
                if kb == 0:
                    pe.wait_ge(ctx_in[j], n["ctx"])
                if kb == KB:
                    pe.wait_ge(tp_act, n["n"] * 6 + 5)
                    for d in range(DC):
                        mm = nc.tensor.transpose(ps[:, 0, d * TAIL:(d + 1) * TAIL],
                                                 cbuf[j][0:TAIL, KT, d * P:(d + 1) * P], ident[0:TAIL, 0:TAIL])
                    mm.then_inc(tp_done, 1)
                    return
                for d in range(DC):
                    if d < 2 and not (first and kb == 0):
                        pe.wait_ge(tp_act, n["n"] * 6 + (2 * kb - 1 + d))
                        if d == 0 and kb == 0:
                            pe.wait_ge(tp_dve, n["n"] * 7)
                    if d >= 2 and not (first and kb == 0):
                        pe.wait_ge(tp_dve, n["n"] * 7 + (2 * kb - 1 + d - 2 - (1 if kb == 0 else 0)))
                    for t in range(4):
                        mm = nc.tensor.transpose(ps[:, d, t * P:(t + 1) * P],
                                                 cbuf[j][:, 4 * kb + t, d * P:(d + 1) * P], ident[:])
                    mm.then_inc(tp_done, 1)

            def scores(n, j, kb, first=False):
                if kb == 0:
                    pe.wait_ge(q_ready, n["n"] + 1)
                if kb == KB:
                    pe.wait_ge(tp_dve, n["n"] * 7 + 7)
                else:
                    pe.wait_ge(tp_act, n["n"] * 6 + (2 * kb + 2))
                    pe.wait_ge(tp_dve, n["n"] * 7 + (2 * kb + 2))
                if not (first and kb < 2):
                    pe.wait_ge(e_evac, n["n"] * 4 + (kb - 1))
                w = TAIL if kb == KB else 512
                for d in range(DC):
                    mm = nc.tensor.matmul(ps[0:S, 4 + kb % 2, 0:w], qs[j][:, d, :], cT[kb % 2][:, d, 0:w],
                                          start=(d == 0), stop=(d == DC - 1))
                mm.then_inc(e_done, 1)

            def spread_length(n, j, first=False):
                pe.wait_ge(cnt_done, n["n"] + 1)
                if not first:
                    pe.wait_ge(o_evac, n["n"])
                nc.tensor.matmul(ps[0:S, 7, 256:257], ones[0:1, 0:S], s_cnt[0:1, j, 0:1],
                                 start=True, stop=True).then_inc(len_done, 1)

            def values(b, j):
                pe.wait_ge(sm_step, b["n"] * 9 + 9)
                for t in range(KT + 1):
                    if t == 8:
                        mm.then_inc(pt_done, 1)
                        pe.wait_ge(pt_evac, b["n"] * 3 + 1)
                    m = P if t < KT else TAIL
                    dst, src = ps[0:m, 6, (t % 8) * S:(t % 8 + 1) * S], es[j][0:S, t * P:t * P + m]
                    if t % 8 == 0:
                        mm = nc.tensor.matmul(dst, src, ident[0:S, 0:S], start=True, stop=True)
                    else:
                        mm = nc.tensor.transpose(dst, src, ident[0:S, 0:S])
                mm.then_inc(pt_done, 1)
                pe.wait_ge(pt_evac, b["n"] * 3 + 3)
                for d in range(DC):
                    for t in range(KT + 1):
                        m = P if t < KT else TAIL
                        mm = nc.tensor.matmul(ps[:, 7, d * S:(d + 1) * S], cbuf[j][0:m, t, d * P:(d + 1) * P],
                                              pts[0:m, t, :], start=(t == 0), stop=(t == KT))
                mm.then_inc(o_done, 1)

            def step(n, b, jn, jb, first=False, last=False):
                if not last:
                    transpose_block(n, jn, 0, first)
                    for kb in range(1, KB + 1):
                        transpose_block(n, jn, kb, first)
                        scores(n, jn, kb - 1, first)
                    scores(n, jn, KB, first)
                if not first:
                    values(b, jb)
                if not last:
                    spread_length(n, jn, first)

            def count(n, ctx):
                return {"n": n, "ctx": ctx}

            step(count(0, 32), None, 0, None, first=True)
            with pe.Fori(0, (B - 1) // CB) as i:
                for j in range(CB):
                    jn = (j + 1) % CB
                    step(count(i * CB + (j + 1), i * 32 + (64 if jn == 0 else 32)), count(i * CB + j, None), jn, j)
            step(None, count(B - 1, None), None, 0, last=True)

            pe.wait_ge(wv2_in, 16)
            pe.wait_ge(o_evac, B)
            for i in range(NT):
                product(("z2", i), 512, [(qT[:, d, tok(i)], wv2[:, d, :]) for d in range(DC)])
            for i in range(NT):
                pe.wait_ge(ln_out, NT + i + 1)
                transpose_rows(("t2", i), hr[:, i, :])
            pe.wait_ge(fc_in, 32)
            for h in range(2):
                for i in range(4 * h, 4 * h + 4):
                    wait_evacuated(pe, "t2", i)
                for c in range(DC):
                    product(("f1", c, h), 512, [(fc1[:, d, tok(c)], hT[:, d, half(h)]) for d in range(DC)])
            for i in range(NT):
                for c in range(DC):
                    wait_evacuated(pe, "f1", c, i // 4)
                product(("f2", i), 512, [(f1T[:, d, tok(i)], fc2[:, d, :]) for d in range(DC)])
            for i in range(NT):
                pe.wait_ge(ln_norm, 4 * NT + i + 1)
                transpose_rows(("t4", i), hr[:, i, :])
            pe.wait_ge(win_in, 16)
            for i in range(NT):
                wait_evacuated(pe, "t4", i)
            for name, base in (("xh", HC), ("ga", 0)):
                for c in range(HC):
                    for h in range(2):
                        product((name, c, h), 512,
                                [(win[:, d, tok(base + c)], hT[:, d, half(h)]) for d in range(DC)])
            pe.wait_ge(wga_in, 16)
            pe.wait_ge(conv_done, HC)
            for c in range(HC):
                for h in range(2):
                    product(("fg", c, h), 512, [(wga[:, k, tok(c)], xhc[:, k, half(h)]) for k in range(HC)])
            for h in range(2):
                for c in range(HC):
                    product(("ig", c, h), 512, [(wga[:, k, tok(HC + c)], xhc[:, k, half(h)]) for k in range(HC)])
            pe.wait_ge(wout_in, 16)
            for i in range(NT):
                pe.wait_ge(gated, HC * (i // 4 + 1))
                product(("wo", i), 512, [(gel[:, k, tok(i)], wout[:, k, :]) for k in range(HC)])
            for i in range(NT):
                pe.wait_ge(ln_norm, 5 * NT + i + 1)
                transpose_rows(("t5", i), hr[:, i, :])
            wait_bank_free(pe, "lg")
            for i in range(NT):
                wait_evacuated(pe, "t5", i)
                for d in range(DC):
                    mm = nc.tensor.matmul(bank("lg")[:, i * NE:(i + 1) * NE], hT[:, d, tok(i)], gwT[:, d, :],
                                          start=(d == 0), stop=(d == DC - 1))
            signals_filled(mm, "lg")
            pe.wait_ge(oh_done, 1)
            wait_bank_free(pe, "rk")
            W = TOPK * NE
            for i in range(NT):
                for k in range(i + 1):
                    mm = nc.tensor.matmul(bank("rk")[:, i * W:(i + 1) * W], (tri if k == i else ones)[:],
                                          oh[:, TOPK * k:TOPK * k + TOPK, :].rearrange("p k e -> p (k e)"),
                                          start=(k == 0), stop=(k == i))
            signals_filled(mm, "rk")

            def slots(s):
                return P if s < NS - 1 else LAST

            def transpose_slots(n, j, s, first=False):
                if s == 0:
                    pe.wait_ge(xe_in[j], n["half"] * 32 + 32)
                if not (first and s == 0):
                    pe.wait_ge(xt_evac, n["n"] * NS + s)
                m = slots(s)
                for d in range(DC):
                    dst, src = ps[:, 7, d * m:(d + 1) * m], xe[j][0:m, s, d * P:(d + 1) * P]
                    if d == 0 and m == LAST:
                        mm = nc.tensor.matmul(dst, src, ident[0:m, 0:m], start=True, stop=True)
                    else:
                        mm = nc.tensor.transpose(dst, src, ident[0:m, 0:m])
                mm.then_inc(xt_done, 1)

            def expert(n, j, nxt, first=False, last=False):
                pe.wait_ge(wgu_in[j], n["half"] * 32 + 32)
                pe.wait_ge(xt_evac, n["n"] * NS + NS)
                for f in range(FC):
                    if not (first and f < 2):
                        pe.wait_ge(hid_done, n["n"] * FC + (f - 1))
                    for w, k in ((wg, 0), (wu, 2)):
                        for d in range(DC):
                            mm = nc.tensor.matmul(ps[:, k + f % 2, 0:SLOTS], w[j][:, d, f * P:(f + 1) * P],
                                                  xeT[j][:, d, :], start=(d == 0), stop=(d == DC - 1))
                        mm.then_inc(gu_done, 1)
                    if f in (3, 5, 7) and not last:
                        transpose_slots(nxt, 1 - j, (f - 3) // 2)
                pe.wait_ge(wd_in[j], n["half"] * 16 + 16)
                for s in range(NS):
                    if not first:
                        pe.wait_ge(y_evac, n["n"] * NS + (s - NS + 1))
                    for f in range(FC):
                        if s == 0:
                            pe.wait_ge(hid_done, n["n"] * FC + (f + 1))
                        m = slots(s)
                        mm = nc.tensor.matmul(ps[0:m, 4 + s, :], hid[j][:, f, s * P:s * P + m], wd[j][:, f, :],
                                              start=(f == 0), stop=(f == FC - 1))
                    mm.then_inc(y_done, 1)

            def nth(n, half):
                return {"n": n, "half": half}

            wait_evacuated(pe, "rk")
            for s in range(NS):
                transpose_slots(nth(0, 0), 0, s, first=True)
            expert(nth(0, 0), 0, nth(1, 0), first=True)
            with pe.Fori(0, NE // 2 - 1) as i:
                expert(nth(i * 2 + 1, i), 1, nth(i * 2 + 2, i + 1))
                expert(nth(i * 2 + 2, i + 1), 0, nth(i * 2 + 3, i + 1))
            expert(nth(NE - 1, NE // 2 - 1), 1, None, last=True)

        @block.scalar
        def _(act):
            def copy_out(dst, src_bank, g):
                wait_filled(act, *g)
                signals_evacuated(nc.scalar.copy(dst, src_bank), *g)

            def transposed_out(name, i):
                copy_out(hT[:, :, i * P:(i + 1) * P], bank(name, i).rearrange("p (c t) -> p c t", t=P), (name, i))

            for c in range(DC):
                copy_out(m1[:, c, :], bank("m1", c), ("m1", c))
            for i in range(NT):
                transposed_out("t0", i)
            for h in range(2):
                for c in range(DC):
                    copy_out(gT[:, c, h * 512:(h + 1) * 512], bank("gt", c, h), ("gt", c, h))
            for i in range(NT):
                copy_out(vv[:, i, :], bank("v", i), ("v", i))
            for c in range(2):
                copy_out(m2[:, c, :], bank("m2", c), ("m2", c))
            for h in range(2):
                act.wait_ge(sa_shift, h + 1)
                hs = slice(4 * h, 4 * h + 4)
                nc.scalar.activation(sP[:, hs, :], sP[:, hs, :], ACT.Exp, scale=SCALE).then_inc(sa_exp, 1)
            for c in range(2, DC):
                copy_out(m2[:, c, :], bank("m2", c), ("m2", c))
            for i in range(NT):
                copy_out(sT[:, i, :], bank("pt", i)[:, 0:P], ("pt", i))
            for i in range(NT):
                transposed_out("t1", i)
            for h in range(2):
                for c in range(DC):
                    copy_out(qT[:, c, h * 512:(h + 1) * 512], bank("q", c, h), ("q", c, h))

            def block_out(n, kb, first=False):
                if not (first and kb < 2):
                    act.wait_ge(e_done, n * 4 + (kb - 1))
                for d in range(2):
                    act.wait_ge(tp_done, n * 13 + (4 * kb + d + 1))
                    nc.scalar.copy(cT[kb % 2][:, d, :], ps[:, d, :]).then_inc(tp_act, 1)

            def scores_out(n, j, kb):
                act.wait_ge(e_done, n * 4 + (kb + 1))
                w = TAIL if kb == KB else 512
                nc.scalar.copy(es[j][0:S, kb * 512:kb * 512 + w], ps[0:S, 4 + kb % 2, 0:w]).then_inc(e_evac, 1)

            def probabilities(b, j):
                act.wait_ge(sm_step, b * 9 + 6)
                nc.scalar.activation(es[j][0:S, :], es[j][0:S, :], ACT.Exp, bias=s_cnt[:, j, 5:6], scale=SCALE,
                                     accum_out=s_cnt[:, j, 6:7]).then_inc(exp_done, 1)

            def step(n, b, jn, jb, first=False, last=False):
                if not last:
                    block_out(n, 0, first)
                    block_out(n, 1, first)
                    scores_out(n, jn, 0)
                if not first:
                    probabilities(b, jb)
                if not last:
                    block_out(n, 2)
                    for kb in range(1, KB + 1):
                        scores_out(n, jn, kb)

            step(0, None, 0, None, first=True)
            with act.Fori(0, (B - 1) // CB) as i:
                for j in range(CB):
                    step(i * CB + (j + 1), i * CB + j, (j + 1) % CB, j)
            step(None, B - 1, None, 0, last=True)

            for i in range(NT):
                transposed_out("t2", i)
            for h in range(2):
                for c in range(DC):
                    wait_filled(act, "f1", c, h)
                    signals_evacuated(nc.scalar.activation(f1T[:, c, h * 512:(h + 1) * 512], bank("f1", c, h),
                                                           ACT.Relu, bias=fc1b[:, c:c + 1]), "f1", c, h)
            act.wait_ge(lac_step, 2)
            nc.scalar.activation(lac[:, 1, :], lac[:, 0, :], ACT.Exp).then_inc(lac_done, 1)
            for i in range(NT):
                transposed_out("t4", i)
            for c in range(HC):
                if c >= 2:
                    act.wait_ge(conv_done, c - 1)
                for h in range(2):
                    copy_out(raw[c % 2][:, h * 512:(h + 1) * 512], bank("xh", c, h), ("xh", c, h))
            for c in range(HC):
                for h in range(2):
                    wait_filled(act, "ga", c, h)
                    signals_evacuated(nc.scalar.activation(gel[:, c, h * 512:(h + 1) * 512], bank("ga", c, h),
                                                           ACT.Gelu), "ga", c, h)
            for c in range(HC):
                for h in range(2):
                    wait_filled(act, "fg", c, h)
                    signals_evacuated(nc.scalar.activation(alp[:, c, h * 512:(h + 1) * 512], bank("fg", c, h),
                                                           ACT.Sigmoid, bias=bgate[:, c:c + 1]), "fg", c, h)
            act.wait_ge(lac_step, LAC_STEPS)
            for c in range(HC):
                for h in range(2):
                    wait_evacuated(act, "fg", c, h)
                nc.scalar.activation(alp[:, c, :], alp[:, c, :], ACT.Exp, scale=lac[:, 7, c:c + 1]).then_inc(alpha_done, 1)
            for c in range(HC):
                act.wait_ge(square_done, c + 1)
                nc.scalar.activation(bet[c], bet[c], ACT.Sqrt, bias=consts[:, 1:2], scale=-1.0).then_inc(beta_done, 1)
            for h in range(2):
                for c in range(HC):
                    k = h * HC + c
                    if k >= 2:
                        act.wait_ge(rec_step, 3 * (k - 2) + 1)
                    wait_filled(act, "ig", c, h)
                    signals_evacuated(nc.scalar.activation(sgi[k % 2], bank("ig", c, h), ACT.Sigmoid,
                                                           bias=bgate[:, HC + c:HC + c + 1]), "ig", c, h)
            for i in range(NT):
                transposed_out("t5", i)
            act.wait_ge(rt_shift, 1)
            nc.scalar.activation(lg[:], lg[:], ACT.Exp).then_inc(rt_exp, 1)

            def silus(n, first=False):
                for f in range(FC):
                    act.wait_ge(gu_done, n * (2 * FC) + (2 * f + 1))
                    if not (first and f < 2):
                        act.wait_ge(hid_done, n * FC + (f - 1))
                    nc.scalar.activation(sg[f % 2], ps[:, f % 2, 0:SLOTS], ACT.Silu).then_inc(silu_done, 1)

            def slots_out(n, j, s):
                m = P if s < NS - 1 else LAST
                act.wait_ge(xt_done, n * NS + (s + 1))
                nc.scalar.copy(xeT[j][:, :, s * P:s * P + m],
                               ps[:, 7, 0:DC * m].rearrange("p (c m) -> p c m", m=m)).then_inc(xt_evac, 1)

            def expert(n, j, first=False, last=False):
                for f in range(FC):
                    act.wait_ge(gu_done, n * (2 * FC) + (2 * f + 1))
                    if not (first and f < 2):
                        act.wait_ge(hid_done, n * FC + (f - 1))
                    nc.scalar.activation(sg[f % 2], ps[:, f % 2, 0:SLOTS], ACT.Silu).then_inc(silu_done, 1)
                    if f in (3, 5, 7) and not last:
                        slots_out(n + 1, 1 - j, (f - 3) // 2)

            for s in range(NS):
                slots_out(0, 0, s)
            expert(0, 0, first=True)
            with act.Fori(0, NE // 2 - 1) as i:
                expert(i * 2 + 1, 1)
                expert(i * 2 + 2, 0)
            expert(NE - 1, 1, last=True)

        @block.vector
        def _(dve):
            V = nc.vector

            def norm_stats(L, i, src):
                n = L * NT + i + 1
                V.bn_stats(stats[:, i, :], src).then_inc(ln_stats, 1)
                dve.wait_ge(ln_stats, n)
                V.bn_aggr(mv[:, i, :], stats[:, i, :]).then_inc(ln_mv, 1)

            def norm_apply(L, i, src):
                dve.wait_ge(ln_rstd, L * NT + i + 1)
                V.tensor_scalar(hr[:, i, :], src, mv[:, i, 0:1], rstd[:, i:i + 1],
                                ALU.subtract, ALU.mult).then_inc(ln_norm, 1)

            def bc(col):
                return col.unsqueeze(2).to_broadcast([P, 4, P])

            def mask4(m):
                return m[:].unsqueeze(1).to_broadcast([P, 4, P])

            for i in range(NT):
                if i % 2 == 0:
                    dve.wait_ge(x_in[i // 2], 16)
                norm_stats(0, i, xr[:, i, :])
                if i:
                    norm_apply(0, i - 1, xr[:, i - 1, :])
            norm_apply(0, NT - 1, xr[:, NT - 1, :])

            dve.wait_ge(consts_in, 16 * 16)
            steps = [0]

            def chained(ins):
                steps[0] += 1
                ins.then_inc(sa_step, 1)
                dve.wait_ge(sa_step, steps[0])

            hs = [slice(0, 4), slice(4, 8)]
            for h in range(2):
                e4 = bank("e", h).rearrange("p (q k) -> p q k", k=P)
                wait_filled(dve, "e", h)
                chained(V.scalar_tensor_tensor(ne[:, hs[h], :], e4, 0.0, mask4(own), ALU.not_equal, ALU.mult))
                signals_evacuated(V.tensor_tensor(sP[:, hs[h], :], e4, mask4(cmask), ALU.add), "e", h)
                V.tensor_reduce(cnt[:, hs[h]], ne[:, hs[h], :], AX_X, ALU.add).then_inc(sa_cnt, 1)
            for h in range(2):
                wait_filled(dve, "len", h)
                signals_evacuated(V.tensor_copy(lens[:, hs[h]], bank("len", h)[:, 0:4]), "len", h)
                wait_evacuated(dve, "len", h)
                chained(V.reciprocal(rlen[:, hs[h]], lens[:, hs[h]]))
                V.tensor_tensor(onel[:, hs[h]], rlen[:, hs[h]], lens[:, hs[h]], ALU.mult).then_inc(sa_step, 1)
                steps[0] += 1
                chained(V.tensor_tensor(pad[:, hs[h], :], mask4(kidx_self), bc(lens[:, hs[h]]), ALU.is_ge))
                chained(V.scalar_tensor_tensor(sP[:, hs[h], :], pad[:, hs[h], :], NEG, sP[:, hs[h], :],
                                               ALU.mult, ALU.add))
                chained(V.tensor_reduce(mx[:, hs[h]], sP[:, hs[h], :], AX_X, ALU.max))
                V.tensor_tensor(sP[:, hs[h], :], sP[:, hs[h], :], bc(mx[:, hs[h]]), ALU.subtract).then_inc(sa_shift, 1)
            for h in range(2):
                dve.wait_ge(sa_exp, h + 1)
                chained(V.tensor_reduce(rsum[:, hs[h]], sP[:, hs[h], :], AX_X, ALU.add))
                chained(V.reciprocal(rinv[:, hs[h]], rsum[:, hs[h]]))
                chained(V.tensor_tensor(rinv[:, hs[h]], rinv[:, hs[h]], onel[:, hs[h]], ALU.mult))
                V.tensor_tensor(sP[:, hs[h], :], sP[:, hs[h], :], bc(rinv[:, hs[h]]), ALU.mult).then_inc(sa_prob, 1)

            added = [0]

            def residual(name, i, into):
                wait_filled(dve, name, i)
                ins = V.tensor_tensor(into, into, bank(name, i), ALU.add)
                signals_evacuated(ins, name, i)
                wait_evacuated(dve, name, i)

            for i in range(NT):
                residual("z", i, hr[:, i, :])
                norm_stats(1, i, hr[:, i, :])
                if i:
                    norm_apply(1, i - 1, hr[:, i - 1, :])
            norm_apply(1, NT - 1, hr[:, NT - 1, :])

            dve.wait_ge(xs_zeroed, 16)

            def block_out(n, kb, first=False):
                if not (first and kb < 2):
                    dve.wait_ge(e_done, n * 4 + (kb - 1))
                if kb == KB:
                    dve.wait_ge(tp_done, n * 13 + 13)
                    V.tensor_copy(cT[kb % 2][:, :, 0:TAIL],
                                  ps[:, 0, 0:DC * TAIL].rearrange("p (c t) -> p c t", t=TAIL)).then_inc(tp_dve, 1)
                    return
                for d in range(2, DC):
                    dve.wait_ge(tp_done, n * 13 + (4 * kb + d + 1))
                    V.tensor_copy(cT[kb % 2][:, d, :], ps[:, d, :]).then_inc(tp_dve, 1)

            def count_keys(n, j):
                dve.wait_ge(e_evac, n * 4 + 4)
                V.tensor_scalar(kpad[0:1, :], es[j][0:1, :], 0.0, None, ALU.not_equal,
                                ALU.add, accum_out=s_cnt[0:1, j, 0:1]).then_inc(cnt_done, 1)

            def shift(b, j):
                c = s_cnt
                dve.wait_ge(len_done, b + 1)
                V.tensor_copy(c[:, j, 1:2], ps[0:S, 7, 256:257]).then_inc(sm_step, 1)
                dve.wait_ge(sm_step, b * 9 + 1)
                V.reciprocal(c[:, j, 2:3], c[:, j, 1:2]).then_inc(sm_step, 1)
                V.tensor_scalar(kpad[0:S, :], kidx[0:S, 0:SK], c[:, j, 1:2], NEG, ALU.is_ge, ALU.mult).then_inc(sm_step, 1)
                dve.wait_ge(sm_step, b * 9 + 3)
                V.tensor_tensor(c[:, j, 3:4], c[:, j, 1:2], c[:, j, 2:3], ALU.mult).then_inc(sm_step, 1)

            def shift_max(b, j):
                c = s_cnt
                V.tensor_tensor_reduce(es[j][0:S, :], es[j][0:S, :], kpad[0:S, :], 1.0, -3e38, ALU.add, ALU.max,
                                       c[:, j, 4:5]).then_inc(sm_step, 1)
                dve.wait_ge(sm_step, b * 9 + 5)
                V.tensor_scalar(c[:, j, 5:6], c[:, j, 4:5], -SCALE, None, ALU.mult).then_inc(sm_step, 1)

            def normalise(b, j):
                c = s_cnt
                dve.wait_ge(exp_done, b + 1)
                V.reciprocal(c[:, j, 7:8], c[:, j, 6:7]).then_inc(sm_step, 1)
                dve.wait_ge(sm_step, b * 9 + 7)
                V.tensor_tensor(c[:, j, 7:8], c[:, j, 7:8], c[:, j, 3:4], ALU.mult).then_inc(sm_step, 1)
                dve.wait_ge(sm_step, b * 9 + 8)
                V.tensor_scalar(es[j][0:S, :], es[j][0:S, :], c[:, j, 7:8], None, ALU.mult).then_inc(sm_step, 1)

            def values_out(b, j):
                dve.wait_ge(pt_done, b * 2 + 1)
                V.tensor_copy(pts[:, 0:8, :], ps[:, 6, :].rearrange("p (t q) -> p t q", q=S)).then_inc(pt_evac, 1)
                dve.wait_ge(pt_done, b * 2 + 2)
                V.tensor_copy(pts[:, 8:KT, :], ps[:, 6, 0:(KT - 8) * S].rearrange("p (t q) -> p t q", q=S))\
                    .then_inc(pt_evac, 1)
                V.tensor_copy(pts[0:TAIL, KT, :], ps[0:TAIL, 6, (KT - 8) * S:(KT - 7) * S]).then_inc(pt_evac, 1)
                dve.wait_ge(o_done, b + 1)
                V.tensor_copy(qT[:, :, bass.ds(b * S, S)],
                              ps[:, 7, 0:DC * S].rearrange("p (c q) -> p c q", q=S)).then_inc(o_evac, 1)

            def step(n, b, jn, jb, first=False, last=False):
                if not last:
                    block_out(n, 0, first)
                if not first:
                    shift(b, jb)
                if not last:
                    block_out(n, 1, first)
                if not first:
                    shift_max(b, jb)
                if not last:
                    block_out(n, 2)
                    block_out(n, KB)
                if not first:
                    normalise(b, jb)
                    values_out(b, jb)
                if not last:
                    count_keys(n, jn)

            step(0, None, 0, None, first=True)
            with dve.Fori(0, (B - 1) // CB) as i:
                for j in range(CB):
                    step(i * CB + (j + 1), i * CB + j, (j + 1) % CB, j)
            step(None, B - 1, None, 0, last=True)

            dve.wait_ge(lnw_in, 16)
            for i in range(NT):
                residual("z2", i, hr[:, i, :])
                norm_stats(2, i, hr[:, i, :])
                if i:
                    norm_apply(2, i - 1, hr[:, i - 1, :])
            norm_apply(2, NT - 1, hr[:, NT - 1, :])

            lsteps = [0]

            def lac_chained(ins):
                lsteps[0] += 1
                ins.then_inc(lac_step, 1)
                dve.wait_ge(lac_step, lsteps[0])

            lac_chained(V.tensor_scalar(lac[:, 1, :], fbase[:], -1.0, None, ALU.mult))
            lac_chained(V.tensor_tensor(lac[:, 0, :], fbase[:], lac[:, 1, :], ALU.min))
            dve.wait_ge(lac_done, 1)
            lac_chained(V.tensor_scalar(lac[:, 2, :], lac[:, 1, :], 2.0, None, ALU.add))
            lac_chained(V.reciprocal(lac[:, 3, :], lac[:, 2, :]))
            lac_chained(V.tensor_tensor(lac[:, 2, :], lac[:, 1, :], lac[:, 3, :], ALU.mult))
            V.tensor_tensor(lac[:, 3, :], lac[:, 2, :], lac[:, 2, :], ALU.mult).then_inc(lac_step, 1)
            V.memset(lac[:, 4, :], 1.0 / (2 * ATANH_TERMS - 1)).then_inc(lac_step, 1)
            lsteps[0] += 2
            dve.wait_ge(lac_step, lsteps[0])
            for k in range(ATANH_TERMS - 2, 0, -1):
                lac_chained(V.tensor_tensor(lac[:, 4, :], lac[:, 4, :], lac[:, 3, :], ALU.mult))
                lac_chained(V.tensor_scalar(lac[:, 4, :], lac[:, 4, :], 1.0 / (2 * k + 1), None, ALU.add))
            lac_chained(V.tensor_tensor(lac[:, 4, :], lac[:, 4, :], lac[:, 3, :], ALU.mult))
            V.tensor_scalar(lac[:, 5, :], fbase[:], 0.0, -8.0, ALU.max, ALU.mult).then_inc(lac_step, 1)
            lsteps[0] += 1
            lac_chained(V.scalar_tensor_tensor(lac[:, 6, :], lac[:, 4, :], 1.0, lac[:, 2, :], ALU.add, ALU.mult))
            lac_chained(V.scalar_tensor_tensor(lac[:, 7, :], lac[:, 6, :], -16.0, lac[:, 5, :], ALU.mult, ALU.add))
            assert lsteps[0] == LAC_STEPS, lsteps

            halves = [0]
            for i in range(NT):
                residual("f2", i, hr[:, i, :])
                V.tensor_tensor(hr[:, i, :], hr[:, i, :], lnw[:, 6, :], ALU.add).then_inc(res_half, 1)
                dve.wait_ge(res_half, i + 1)
                norm_stats(3, i, hr[:, i, :])
                if i:
                    norm_apply(3, i - 1, hr[:, i - 1, :])
            norm_apply(3, NT - 1, hr[:, NT - 1, :])
            for i in range(NT):
                dve.wait_ge(ln_out, 2 * NT + i + 1)
                V.tensor_tensor(xr[:, i, :], xr[:, i, :], hr[:, i, :], ALU.add).then_inc(res_sum, 1)
                dve.wait_ge(res_sum, i + 1)
                norm_stats(4, i, xr[:, i, :])
                if i:
                    norm_apply(4, i - 1, xr[:, i - 1, :])
            norm_apply(4, NT - 1, xr[:, NT - 1, :])

            for c in range(HC):
                src = raw[c % 2].rearrange("p (b s) -> p b s", s=S)
                dst = xhc[:, c, :].rearrange("p (b s) -> p b s", s=S)
                for h in range(2):
                    wait_evacuated(dve, "xh", c, h)
                V.tensor_scalar(xhc[:, c, :], raw[c % 2], convw[:, c, 3:4], convb[:, c:c + 1],
                                ALU.mult, ALU.add).then_inc(conv_step, 1)
                for k in range(3):
                    back = 3 - k
                    dve.wait_ge(conv_step, 3 * c + k + 1)
                    V.scalar_tensor_tensor(dst[:, :, back:S], src[:, :, 0:S - back], convw[:, c, k:k + 1],
                                           dst[:, :, back:S], ALU.mult, ALU.add)\
                        .then_inc(conv_step if k < 2 else conv_done, 1)
            for c in range(HC):
                dve.wait_ge(alpha_done, c + 1)
                V.tensor_tensor(bet[c], alp[:, c, :], alp[:, c, :], ALU.mult).then_inc(square_done, 1)
                dve.wait_ge(square_done, c + 1)
                V.memset(alp[:, c, :].rearrange("p (b s) -> p b s", s=S)[:, :, 0:1], 0.0).then_inc(alpha_reset, 1)
            for h in range(2):
                for c in range(HC):
                    k = h * HC + c
                    cols = slice(h * 512, (h + 1) * 512)
                    wait_evacuated(dve, "ig", c, h)
                    dve.wait_ge(beta_done, c + 1)
                    V.tensor_tensor(bet[c][:, cols], bet[c][:, cols], sgi[k % 2], ALU.mult).then_inc(rec_step, 1)
                    dve.wait_ge(rec_step, 3 * k + 1)
                    V.tensor_tensor(bet[c][:, cols], bet[c][:, cols], xhc[:, c, cols], ALU.mult).then_inc(rec_step, 1)
                    dve.wait_ge(rec_step, 3 * k + 2)
                    dve.wait_ge(alpha_reset, c + 1)
                    V.tensor_tensor_scan(bet[c][:, cols], alp[:, c, cols], bet[c][:, cols], 0.0,
                                         ALU.mult, ALU.add).then_inc(rec_step, 1)
                    dve.wait_ge(rec_step, 3 * k + 3)
                    V.tensor_tensor(gel[:, c, cols], gel[:, c, cols], bet[c][:, cols], ALU.mult).then_inc(gated, 1)

            for i in range(NT):
                residual("wo", i, xr[:, i, :])
                norm_stats(5, i, xr[:, i, :])
                if i:
                    norm_apply(5, i - 1, xr[:, i - 1, :])
            norm_apply(5, NT - 1, xr[:, NT - 1, :])

            rsteps = [0]

            def rt_chained(ins):
                rsteps[0] += 1
                ins.then_inc(rt_step, 1)
                dve.wait_ge(rt_step, rsteps[0])

            def over_e(col, n=NT):
                return col.unsqueeze(2).to_broadcast([P, n, NE])

            wait_filled(dve, "lg")
            signals_evacuated(V.tensor_copy(lg[:], bank("lg")[:, 0:NT * NE].rearrange("p (i e) -> p i e", e=NE)), "lg")
            wait_evacuated(dve, "lg")
            rt_chained(V.tensor_reduce(mx[:], lg[:], AX_X, ALU.max))
            V.tensor_tensor(lg[:], lg[:], over_e(mx[:]), ALU.subtract).then_inc(rt_shift, 1)
            dve.wait_ge(rt_exp, 1)
            rt_chained(V.tensor_reduce(rsum[:], lg[:], AX_X, ALU.add))
            rt_chained(V.reciprocal(rinv[:], rsum[:]))
            rt_chained(V.tensor_tensor(lg[:], lg[:], over_e(rinv[:]), ALU.mult))
            for i in range(NT):
                rt_chained(V.max(top8[:, i, :], lg[:, i, :]))
                rt_chained(V.max_index(topi[:, i, :], top8[:, i, :], lg[:, i, :]))
            r3 = [rt[:, k, :].rearrange("p (i k) -> p i k", k=TOPK) for k in range(8)]
            rt_chained(V.tensor_copy(r3[0], topi[:, :, 0:TOPK]))
            V.tensor_tensor(oh[:], eidx[:], over_e(rt[:, 0, :], NT * TOPK), ALU.is_equal).then_inc(oh_done, 1)
            dve.wait_ge(oh_done, 1)
            rt_chained(V.tensor_tensor(rsum[:], top8[:, :, 0], top8[:, :, 1], ALU.add))
            rt_chained(V.tensor_scalar(rsum[:], rsum[:], 1e-9, None, ALU.add))
            rt_chained(V.reciprocal(rinv[:], rsum[:]))
            rt_chained(V.tensor_tensor(r3[1], top8[:, :, 0:TOPK], rinv[:].unsqueeze(2).to_broadcast([P, NT, TOPK]),
                                       ALU.mult))
            rt_chained(V.scalar_tensor_tensor(rt[:, 2, :], rt[:, 0, :], float(SLOTS), slot_at[:, 0, :],
                                              ALU.mult, ALU.add))
            wait_filled(dve, "rk")
            signals_evacuated(V.tensor_tensor(
                rk[:], bank("rk")[:, 0:NT * TOPK * NE].rearrange("p (i e) -> p i e", e=NE), oh[:], ALU.mult), "rk")
            wait_evacuated(dve, "rk")
            rt_chained(V.tensor_reduce(rt[:, 3, :], rk[:], AX_X, ALU.add))
            rt_chained(V.tensor_scalar(rt[:, 4, :], rt[:, 3, :], float(CAP), None, ALU.is_le))
            rt_chained(V.tensor_tensor(rt[:, 5, :], rt[:, 3, :], rt[:, 2, :], ALU.add))
            rt_chained(V.tensor_tensor(rt[:, 1, :], rt[:, 1, :], rt[:, 4, :], ALU.mult))
            rt_chained(V.tensor_tensor(rt[:, 6, :], rt[:, 5, :], rt[:, 4, :], ALU.mult))
            rt_chained(V.tensor_tensor(rt[:, 5, :], rt[:, 5, :], slot_at[:, 1, :], ALU.subtract))
            rt_chained(V.tensor_tensor(rt[:, 5, :], rt[:, 5, :], rt[:, 4, :], ALU.mult))
            rt_chained(V.tensor_tensor(rt[:, 5, :], rt[:, 5, :], slot_at[:, 1, :], ALU.add))
            V.tensor_copy(scat[:], rt[:, 5, :]).then_inc(idx_done, 1)
            V.tensor_copy(gath[:], rt[:, 6, :]).then_inc(idx_done, 1)

            def expert(n, j, half, first=False):
                for f in range(FC):
                    dve.wait_ge(gu_done, n * (2 * FC) + (2 * f + 2))
                    dve.wait_ge(silu_done, n * FC + (f + 1))
                    V.tensor_tensor(hid[j][:, f, :], sg[f % 2], ps[:, 2 + f % 2, 0:SLOTS], ALU.mult).then_inc(hid_done, 1)
                for s in range(NS):
                    dve.wait_ge(y_done, n * NS + (s + 1))
                    if s == 0 and half is not None:
                        dve.wait_ge(y_out[j], half * 32)
                    m = P if s < NS - 1 else LAST
                    V.tensor_copy(ye[j][0:m, s, :], ps[0:m, 4 + s, :]).then_inc(y_evac, 1)

            expert(0, 0, None, first=True)
            expert(1, 1, None)
            with dve.Fori(0, NE // 2 - 1) as i:
                expert(i * 2 + 2, 0, i + 1)
                expert(i * 2 + 3, 1, i + 1)

            for i in range(NT):
                dve.wait_ge(yg_in[i % 2], 32 * (i // 2 + 1))
                for k in range(TOPK):
                    V.scalar_tensor_tensor(xr[:, i, :], yg[i % 2][:, k, :], rt[:, 1, TOPK * i + k:TOPK * i + k + 1],
                                           xr[:, i, :], ALU.mult, ALU.add).then_inc(mix_step if k == 0 else out_ready, 1)
                    if k == 0:
                        dve.wait_ge(mix_step, i + 1)

        @block.gpsimd
        def _(pool):
            G = nc.gpsimd
            G.memset(consts[:, 0:1], -0.5).then_inc(consts_set, 1)
            G.memset(consts[:, 1:2], 1.0 + 1e-6).then_inc(consts_set, 1)
            G.memset(zeros, 0.0).then_inc(zero_set, 1)
            pool.wait_ge(zero_set, 1)
            pool.dma_start(xs[0:TRASH, :].rearrange("(r p) d -> p r d", p=P),
                           zeros.unsqueeze(1).to_broadcast([P, TRASH // P, D])).then_inc(xs_zeroed, 16)
            pool.wait_ge(consts_set, 2)

            def norm_scale(L, i):
                n = L * NT + i + 1
                pool.wait_ge(ln_mv, n)
                G.tensor_scalar(veps[:, i:i + 1], mv[:, i, 1:2], EPS, None, ALU.add).then_inc(ln_veps, 1)
                pool.wait_ge(ln_veps, n)
                G.tensor_tensor(rstd[:, i:i + 1], veps[:, i:i + 1], consts[:, 0:1], ALU.pow).then_inc(ln_rstd, 1)

            def gain_and_bias(L, i):
                w = 2 * (L - 1)
                pool.wait_ge(ln_norm, L * NT + i + 1)
                G.tensor_tensor(hr[:, i, :], hr[:, i, :], lnw[:, w, :], ALU.mult).then_inc(ln_gain, 1)
                pool.wait_ge(ln_gain, (L - 1) * NT + i + 1)
                G.tensor_tensor(hr[:, i, :], hr[:, i, :], lnw[:, w + 1, :], ALU.add).then_inc(ln_out, 1)

            def norms(L, gained):
                for i in range(NT):
                    norm_scale(L, i)
                    if gained and i:
                        gain_and_bias(L, i - 1)
                if gained:
                    gain_and_bias(L, NT - 1)

            norms(0, False)
            pool.wait_ge(lnw_in, 16)
            norms(1, True)

            for h in range(2):
                for c in range(DC):
                    wait_evacuated(pool, "q", c, h)

            def queries(n, j):
                G.tensor_copy(qs[j], qT[:, :, bass.ds(n * S, S)]).then_inc(q_ready, 1)

            for j in range(CB):
                queries(j, j)
            with pool.Fori(0, (B - 1) // CB - 1) as i:
                for j in range(CB):
                    pool.wait_ge(e_done, i * (4 * CB) + (4 * j + 4))
                    queries(i * CB + (CB + j), j)
            pool.wait_ge(e_done, 4 * (B - CB))
            queries(B - 1, 0)

            norms(2, True)
            norms(3, True)
            norms(4, False)
            norms(5, False)

            pool.wait_ge(idx_done, 2)
            pool.wait_ge(ln_norm, 6 * NT)
            pool.wait_ge(xs_zeroed, 16)
            for i in range(NT):
                for k in range(TOPK):
                    G.indirect_dma_start(xs, bass.IndirectOffsetOnAxis(scat[:, TOPK * i + k:TOPK * i + k + 1], 0),
                                         hr[:, i, :], None).then_inc(scattered, 16)

            def store(n, j):
                pool.wait_ge(y_evac, n * NS + NS)
                rows = ys[bass.ds(n * SLOTS, SLOTS), :]
                pool.dma_start(rows[0:(NS - 1) * P, :].rearrange("(s p) d -> p s d", p=P),
                               ye[j][:, 0:NS - 1, :]).then_inc(y_out[j], 16)
                pool.dma_start(rows[(NS - 1) * P:SLOTS, :], ye[j][0:LAST, NS - 1, :]).then_inc(y_out[j], 16)

            with pool.Fori(0, NE // 2) as i:
                for j in range(2):
                    store(i * 2 + j, j)
            for j in range(2):
                pool.wait_ge(y_out[j], 32 * (NE // 2))
            for i in range(NT):
                if i >= 2:
                    pool.wait_ge(out_ready, i - 1)
                for k in range(TOPK):
                    G.indirect_dma_start(yg[i % 2][:, k, :], None, ys,
                                         bass.IndirectOffsetOnAxis(gath[:, TOPK * i + k:TOPK * i + k + 1], 0))\
                        .then_inc(yg_in[i % 2], 16)


_OUT = "out"


def kernel(**inputs):
    import numpy as np
    import concourse.bacc as bacc
    from concourse.bass_utils import run_bass_kernel_spmd as run

    v = {k: np.asarray(x) for k, x in inputs.items()}
    f = np.float32

    def cols(w, n):
        return np.ascontiguousarray(w.reshape(n, P).T)

    rows, keys = np.arange(P)[:, None], np.arange(P)[None, :]
    same = (rows // S) == (keys // S)
    t_of = (np.arange(NT)[None, :, None] * P + np.arange(P)[:, None, None])
    k_of = np.arange(TOPK)[None, None, :]
    kidx = np.concatenate([(np.arange(P)[None, :] * KT + np.arange(KT)[:, None]).reshape(-1), np.arange(KT * P, SK)])
    arrays = {
        "x": v["x"].reshape(T, D), "ctx": v["ctx_1024"],
        "wq1T": v["L0_xattn_Wq1"].T, "wk1T": v["L0_xattn_Wk1"].T, "wv1": v["L0_xattn_Wv1"],
        "wq2T": v["L0_xattn_Wq2"].T, "wk2T": v["L0_xattn_Wk2"].T, "wv2": v["L0_xattn_Wv2"],
        "fc1_w": v["L0_xattn_fc1_w"], "fc2_w": v["L0_xattn_fc2_w"],
        "lnw": np.stack([v["L0_xattn_" + n] for n in ("ln1_g", "ln1_b", "ln2_g", "ln2_b", "ln3_g", "ln3_b", "fc2_b")]),
        "fc1b": cols(v["L0_xattn_fc1_b"], DC),
        "w_inT": v["L0_attn_W_in"].T, "w_gatesT": v["L0_attn_W_gates"].T, "w_outT": v["L0_attn_W_out"].T,
        "convw": v["L0_attn_conv_w"].reshape(HC, P, 4).transpose(1, 0, 2), "convb": cols(v["L0_attn_conv_b"], HC),
        "bgate": cols(v["L0_attn_b_gates"], 2 * HC), "fbase": cols(v["L0_attn_forget_base"], HC),
        "gwT": v["L0_ffn_gate_w"].T.reshape(DC, P, NE).transpose(1, 0, 2),
        "w_gate": v["L0_ffn_gate_proj_w"].transpose(0, 2, 1), "w_up": v["L0_ffn_up_proj_w"].transpose(0, 2, 1),
        "w_down": v["L0_ffn_down_proj_w"].transpose(0, 2, 1),
        "ident": np.eye(P, dtype=f), "own": same.astype(f),
        "cmask": np.where(same & (keys <= rows), f(0), f(NEG)), "kidx_self": np.broadcast_to(keys % S, (P, P)).astype(f),
        "sel": (rows == (keys // S) * S).astype(f), "tri": (rows <= keys).astype(f), "ones": np.ones((P, P), f),
        "slot_at": np.stack([np.broadcast_to(CAP * k_of - 1, (P, NT, TOPK)), TRASH + T * k_of + t_of], 1)
        .reshape(P, 2, NT * TOPK).astype(f),
        "eidx": np.broadcast_to(np.arange(NE), (P, NT * TOPK, NE)).astype(f),
        "kidx": np.broadcast_to(kidx, (S, SK)).astype(np.int16),
    }
    arrays = {k: np.ascontiguousarray(x) for k, x in arrays.items()}
    nc = bacc.Bacc("TRN2", target_bir_lowering=False, num_devices=1)
    a = {k: nc.dram_tensor("in_" + k, x.shape, mybir.dt.from_np(x.dtype), kind="ExternalInput").ap() for k, x in arrays.items()}
    out = nc.dram_tensor(_OUT, (T, D), F32, kind="ExternalOutput").ap()
    perceiver_program(nc, a, out)
    r = run(nc, [{"in_" + k: x for k, x in arrays.items()}], core_ids=[0])
    return r.results[0][_OUT].reshape(B, S, D)
```

```python
from contextlib import ExitStack

import concourse.bass as bass
from concourse import mybir
from concourse.alu_op_type import AluOpType as ALU

ACT = mybir.ActivationFunctionType
AX_X = mybir.AxisListType.X
F32 = mybir.dt.float32
U32 = mybir.dt.uint32
F32R = mybir.dt.float32r
I16 = mybir.dt.int16

P = 128
B, S, D = 16, 64, 512
T = B * S
NT = T // P
DC = D // P
SK = 1601
KT = SK // P
TAIL = SK - KT * P
KB = KT // 4
HID = 768
HC = HID // P
NE, TOPK, FF = 8, 2, 1024
FC = FF // P
CAP = int(1.25 * T / NE)
SLOTS = TOPK * CAP
NS = -(-SLOTS // P)
RING, AHEAD = 4, 3
LAST = SLOTS - (NS - 1) * P
TRASH = NE * SLOTS
EPS = 1e-5
SCALE = float((D // 16) ** -0.5)
NEG = -1e38
CB = 2
ATANH_TERMS = 9


def dense_groups():
    g = [("m1", c) for c in range(DC)]
    g += [("t0", i) for i in range(NT)]
    g += [("gt", c, h) for h in range(2) for c in range(DC)]
    g += [("e", h) for h in range(2)]
    g += [("v", i) for i in range(NT)]
    g += [("len", h) for h in range(2)]
    g += [("m2", c) for c in range(DC)]
    g += [("pt", i) for i in range(NT)]
    g += [("z", i) for i in range(NT)]
    g += [("t1", i) for i in range(NT)]
    g += [("q", c, h) for h in range(2) for c in range(DC)]
    g += [("z2", i) for i in range(NT)]
    g += [("t2", i) for i in range(NT)]
    g += [("f1", c, h) for h in range(2) for c in range(DC)]
    g += [("f2", i) for i in range(NT)]
    g += [("t4", i) for i in range(NT)]
    g += [("xh", c, h) for c in range(HC) for h in range(2)]
    g += [("ga", c, h) for c in range(HC) for h in range(2)]
    g += [("fg", c, h) for c in range(HC) for h in range(2)]
    g += [("ig", c, h) for h in range(2) for c in range(HC)]
    g += [("wo", i) for i in range(NT)]
    g += [("t5", i) for i in range(NT)]
    g += [("lg",), ("rk",)]
    return g


def perceiver_program(nc, a, out):
    with ExitStack() as ctx:
        def sb(name, shape, dt=F32):
            return ctx.enter_context(nc.sbuf_tensor(name, shape, dt))

        def sem(name):
            return ctx.enter_context(nc.semaphore(name))

        ps = ctx.enter_context(nc.psum_tensor("ps", [P, 8, 512], F32))
        group_at = {name: (g % 8, g // 8) for g, name in enumerate(dense_groups())}
        filled = [sem(f"filled{k}") for k in range(8)]
        evacuated = [sem(f"evacuated{k}") for k in range(8)]

        def bank(*g):
            return ps[:, group_at[g][0], :]

        def wait_bank_free(pe, *g):
            k, use = group_at[g]
            if use:
                pe.wait_ge(evacuated[k], use)

        def wait_filled(eng, *g):
            eng.wait_ge(filled[group_at[g][0]], group_at[g][1] + 1)

        def wait_evacuated(eng, *g):
            eng.wait_ge(evacuated[group_at[g][0]], group_at[g][1] + 1)

        def signals_filled(ins, *g):
            ins.then_inc(filled[group_at[g][0]], 1)

        def signals_evacuated(ins, *g):
            ins.then_inc(evacuated[group_at[g][0]], 1)

        BIG = 39016
        base = -(-nc.sbuf_base // 32) * 32
        big = sb("big", [P, BIG])
        xr = sb("xr", [P, NT, D])
        hr = sb("hr", [P, NT, D])
        ident = sb("ident", [P, P])
        own = sb("own", [P, P])
        cmask = sb("cmask", [P, P])
        kidx_self = sb("kidx_self", [P, P])
        sel = sb("sel", [P, P])
        tri = sb("tri", [P, P])
        ones = sb("ones", [P, P])
        lnw = sb("lnw", [P, 7, D])
        stats = sb("stats", [P, NT, 6])
        mv = sb("mv", [P, NT, 2])
        veps = sb("veps", [P, NT])
        rstd = sb("rstd", [P, NT])
        consts = sb("consts", [P, 2])
        cnt = sb("cnt", [P, NT])
        lens = sb("lens", [P, NT])
        rlen = sb("rlen", [P, NT])
        onel = sb("onel", [P, NT])
        mx = sb("mx", [P, NT])
        rsum = sb("rsum", [P, NT])
        rinv = sb("rinv", [P, NT])
        fc1b = sb("fc1b", [P, DC])
        convw = sb("convw", [P, HC, 4])
        convb = sb("convb", [P, HC])
        bgate = sb("bgate", [P, 2 * HC])
        fbase = sb("fbase", [P, HC])
        lac = sb("lac", [P, 8, HC])
        gwT = sb("gwT", [P, DC, NE])
        slot_at = sb("slot_at", [P, 2, NT * TOPK])
        eidx = sb("eidx", [P, NT * TOPK, NE])
        lg = sb("lg", [P, NT, NE])
        top8 = sb("top8", [P, NT, 8])
        topi = sb("topi", [P, NT, 8], U32)
        oh = sb("oh", [P, NT * TOPK, NE])
        rk = sb("rk", [P, NT * TOPK, NE])
        rt = sb("rt", [P, 8, NT * TOPK])
        scat = sb("scat", [P, NT * TOPK], U32)
        gath = sb("gath", [P, NT * TOPK], U32)
        s_cnt = sb("s_cnt", [S, CB, 8])
        def at(off, *shape):
            n = 1
            for x in shape:
                n *= x
            assert off + n <= BIG, (off, shape)
            v = big[:, off:off + n]
            if len(shape) == 2:
                v = v.rearrange("p (a b) -> p a b", b=shape[1])
            return v

        def rounded(name, off, *shape):
            n = 1
            for x in shape:
                n *= x
            assert off + n <= BIG, (off, shape)
            return nc.alloc_sbuf_tensor_at(name, [P, *shape], F32R, offset=base + 4 * off)

        HT = 34920
        hT = at(HT, DC, T)
        wq1T, wk1T, m1 = at(6656, DC, D), at(8704, DC, D), at(10752, DC, D)
        wq2T, wk2T, gT = at(12800, DC, D), at(14848, DC, D), at(27712, DC, T)
        wv1, sP, m2, vv = at(31808, DC, D), at(33856, NT, P), at(21504, DC, D), at(17408, NT, D)
        ne, pad, sT = at(6656, NT, P), at(7680, NT, P), at(8704, NT, P)
        zeros = at(24300, D)
        CW = (KT + 1) * D
        cbuf = [at(j * CW, KT + 1, D) for j in range(CB)]
        qT = at(13312, DC, T)
        es = [at(17408 + j * (SK + 1), SK) for j in range(CB)]
        pts = at(20612, KT + 1, S)
        qs = [rounded(f"qs{j}", 21448 + j * DC * P, DC, P) for j in range(CB)]
        qf = [at(31808 + j * 256, DC, S) for j in range(CB)]
        osb = at(22472, D)
        kpad, kidx, wv2 = at(23240, SK), at(24848, 801).bitcast(I16), at(25656, DC, D)
        cT = [[rounded(f"cT{j}{part}", (HT, 27712)[j] + part * DC * 512, DC, 512) for part in range(2)]
              for j in range(2)]
        fc1, fc2, f1T = at(0, DC, D), at(2048, DC, D), at(17408, DC, T)
        wout, wga, win, alp = at(0, HC, D), at(4096, HC, 2 * HID), at(27712, DC, 2 * HID), at(27712, HC, T)
        xhc, gel = at(13312, HC, T), at(19456, HC, T)
        bet = [at(o, T) for o in (25600, 26624, 33856, HT, HT + 1024, HT + 2048)]
        hflat = hr[:].rearrange("p i d -> p (i d)")
        raw = [hflat[:, j * T:(j + 1) * T] for j in range(2)]
        sgi = [hflat[:, 2 * T + j * 512:2 * T + (j + 1) * 512] for j in range(2)]
        UW = (2 * DC) * P + D
        wraw = [at(4096 + j * UW, UW) for j in range(RING)]
        wsplit = [[rounded(f"w{j}{part}", 13312 + (2 * j + part) * UW, UW) for part in range(2)] for j in range(RING)]
        sg = [at(25600 + j * SLOTS, SLOTS) for j in range(2)]
        hid = [at(26240 + j * SLOTS, SLOTS) for j in range(2)]
        hsplit = [rounded(f"hsplit{j}", 26880 + j * 2 * SLOTS, 2 * SLOTS) for j in range(2)]
        xsplit = [[rounded(f"x{j}{part}", 28800 + (2 * j + part) * DC * SLOTS, DC, SLOTS) for part in range(2)]
                  for j in range(2)]
        yg = [at(33920 + j * 2 * D, TOPK, D) for j in range(4)]
        ytail = at(38016, D)
        ye = [at(j * NS * D, NS, D) for j in range(2)]
        xe = [hflat[:, j * NS * D:(j + 1) * NS * D].rearrange("p (s d) -> p s d", d=D) for j in range(2)]

        xs = nc.dram_tensor("xs", (TRASH + TOPK * T, D), F32, kind="Internal").ap()
        ys = nc.dram_tensor("ys", (TRASH, D), F32, kind="Internal").ap()

        x_in = [sem(f"x_in{j}") for j in range(4)]
        consts_in, lnw_in, wq1_in, wq2_in, wv1_in = map(sem, ("consts_in", "lnw_in", "wq1_in", "wq2_in", "wv1_in"))
        wv2_in, fc_in, win_in, wga_in, wout_in = map(sem, ("wv2_in", "fc_in", "win_in", "wga_in", "wout_in"))
        zero_set, xs_zeroed, consts_set = sem("zero_set"), sem("xs_zeroed"), sem("consts_set")
        ln_stats, ln_mv, ln_veps, ln_rstd, ln_norm, ln_gain, ln_out = map(
            sem, ("ln_stats", "ln_mv", "ln_veps", "ln_rstd", "ln_norm", "ln_gain", "ln_out"))
        res_sum, res_half = sem("res_sum"), sem("res_half")
        sa_step, sa_cnt, sa_shift, sa_exp, sa_prob = map(sem, ("sa_step", "sa_cnt", "sa_shift", "sa_exp", "sa_prob"))
        ctx_in = [[sem(f"ctx_in{j}_{kb}") for kb in range(KB + 1)] for j in range(CB)]
        q_high, q_ready, tp_done, tp_high, tp_low, e_done, e_high, e_evac = map(
            sem, ("q_high", "q_ready", "tp_done", "tp_high", "tp_low", "e_done", "e_high", "e_evac"))
        cnt_ne, cnt_done, len_done, sm_step, exp_done = map(sem, ("cnt_ne", "cnt_done", "len_done", "sm_step", "exp_done"))
        pt_done, pt_evac, pv_done, o_copied, o_done, o_evac = map(
            sem, ("pt_done", "pt_evac", "pv_done", "o_copied", "o_done", "o_evac"))
        conv_step, conv_done, lac_step, lac_done = map(sem, ("conv_step", "conv_done", "lac_step", "lac_done"))
        alpha_done, square_done, alpha_reset, beta_done = map(sem, ("alpha_done", "square_done", "alpha_reset", "beta_done"))
        rec_step, gated = sem("rec_step"), sem("gated")
        rt_shift, rt_exp, rt_step, oh_done, idx_done = map(sem, ("rt_shift", "rt_exp", "rt_step", "oh_done", "idx_done"))
        scattered = sem("scattered")
        w_in = [sem(f"w_in{j}") for j in range(RING)]
        xe_in = [sem(f"xe_in{j}") for j in range(2)]
        w_high, w_low, xt_done, xt_high, xt_low = map(sem, ("w_high", "w_low", "xt_done", "xt_high", "xt_low"))
        gu_done, silu_done, hid_done, hid_high, hid_low, down_done, tail_high, y_evac = map(
            sem, ("gu_done", "silu_done", "hid_done", "hid_high", "hid_low", "down_done", "tail_high", "y_evac"))
        y_out = [sem(f"y_out{j}") for j in range(2)]
        y_all = sem("y_all")
        yg_in = [sem(f"yg_in{j}") for j in range(4)]
        mix_step, out_ready, out_done = map(sem, ("mix_step", "out_ready", "out_done"))

        LAC_STEPS = 2 + 3 + 2 + 2 * (ATANH_TERMS - 2) + 4

        block = ctx.enter_context(nc.Block())

        @block.sync
        def _(sp):
            def load(dst, src, signal):
                sp.dma_start(dst, src).then_inc(signal, 16)

            def weights(dst, src, signal):
                load(dst, src.rearrange("(c p) n -> p c n", p=P), signal)

            x_rows = a["x"].rearrange("(i p) d -> p i d", p=P)
            load(xr[:, 0:2, :], x_rows[:, 0:2, :], x_in[0])
            weights(wq1T, a["wq1T"], wq1_in)
            weights(wk1T, a["wk1T"], wq1_in)
            for j in range(1, 4):
                load(xr[:, 2 * j:2 * j + 2, :], x_rows[:, 2 * j:2 * j + 2, :], x_in[j])
            for t, name in ((ident, "ident"), (own, "own"), (cmask, "cmask"), (kidx_self, "kidx_self"),
                            (sel, "sel"), (tri, "tri"), (ones, "ones"), (convw, "convw"), (fc1b, "fc1b"),
                            (convb, "convb"), (bgate, "bgate"), (fbase, "fbase"), (gwT, "gwT"),
                            (slot_at, "slot_at"), (eidx, "eidx")):
                load(t[:], a[name], consts_in)
            load(kidx[0:S, 0:SK], a["kidx"], consts_in)
            weights(wv1, a["wv1"], wv1_in)
            weights(wq2T, a["wq2T"], wq2_in)
            weights(wk2T, a["wk2T"], wq2_in)
            load(lnw[:], a["lnw"].partition_broadcast(P), lnw_in)
            weights(wv2, a["wv2"], wv2_in)

            def load_context(n, j, kb):
                rows = a["ctx"][bass.ds(n, 1), :, :].rearrange("o k d -> (o k) d")
                if kb == KB:
                    load(cbuf[j][0:TAIL, KT, :], rows[KT * P:SK, :], ctx_in[j][kb])
                else:
                    load(cbuf[j][:, 4 * kb:4 * kb + 4, :],
                         rows[0:KT * P, :].rearrange("(p k) d -> p k d", k=KT)[:, 4 * kb:4 * kb + 4, :], ctx_in[j][kb])

            for kb in range(KB + 1):
                load_context(0, 0, kb)
            for h in range(2):
                for c in range(DC):
                    wait_evacuated(sp, "q", c, h)
            for kb in range(KB + 1):
                load_context(1, 1, kb)
            with sp.Fori(0, B // CB - 1) as i:
                for j in range(CB):
                    for kb in range(KB + 1):
                        sp.wait_ge(pv_done, i * (CB * (KB + 1)) + (j * (KB + 1) + kb + 1))
                        load_context(i * CB + (CB + j), j, kb)
            sp.wait_ge(pv_done, (B - 1) * (KB + 1))
            weights(fc1, a["fc1_w"], fc_in)
            weights(fc2, a["fc2_w"], fc_in)
            sp.wait_ge(e_done, B * (KB + 1))
            weights(win, a["w_inT"], win_in)
            sp.wait_ge(pv_done, B * (KB + 1))
            weights(wga, a["w_gatesT"], wga_in)
            for i in range(NT):
                wait_filled(sp, "f2", i)
            weights(wout, a["w_outT"], wout_in)

            def load_unit(n, f, first=False):
                if not first:
                    sp.wait_ge(w_low, n * FC + (f - RING + 1))
                load(wraw[f % RING], a["w_units"][bass.ds(n * FC + f, 1), :, :].rearrange("o p w -> (o p) w"),
                     w_in[f % RING])

            def load_rows(n, j):
                rows = xs[bass.ds(n * SLOTS, SLOTS), :]
                load(xe[j][:, 0:NS - 1, :], rows[0:(NS - 1) * P, :].rearrange("(s p) d -> p s d", p=P), xe_in[j])
                load(xe[j][0:LAST, NS - 1, :], rows[(NS - 1) * P:SLOTS, :], xe_in[j])

            for c in range(HC):
                for h in range(2):
                    wait_filled(sp, "ig", c, h)
            for f in range(RING):
                load_unit(0, f, first=True)
            for i in range(NT):
                wait_filled(sp, "wo", i)
            sp.wait_ge(scattered, 16 * NT * TOPK)
            load_rows(0, 0)
            load_rows(1, 1)
            for f in range(RING, FC):
                load_unit(0, f)

            def expert_loads(n, j, last=False):
                for f in range(FC):
                    load_unit(n, f)
                    if f == 0 and not last:
                        sp.wait_ge(xt_done, n * NS)
                        load_rows(n + 1, 1 - j)

            with sp.Fori(0, NE // 2 - 1) as i:
                expert_loads(i * 2 + 1, 1)
                expert_loads(i * 2 + 2, 0)
            expert_loads(NE - 1, 1, last=True)
            out_rows = out.rearrange("(i p) d -> p i d", p=P)
            for i in range(NT):
                sp.wait_ge(out_ready, i + 1)
                sp.dma_start(out_rows[:, i, :], xr[:, i, :]).then_inc(out_done, 16)
            sp.wait_ge(out_done, 16 * NT)

        @block.tensor
        def _(pe):
            def product(g, cols, pairs):
                wait_bank_free(pe, *g)
                for k, (lhsT, rhs) in enumerate(pairs):
                    mm = nc.tensor.matmul(bank(*g)[:, 0:cols], lhsT, rhs, start=(k == 0), stop=(k == len(pairs) - 1))
                signals_filled(mm, *g)

            def transpose_rows(g, rows):
                wait_bank_free(pe, *g)
                for c in range(DC):
                    mm = nc.tensor.transpose(bank(*g)[:, c * P:(c + 1) * P], rows[:, c * P:(c + 1) * P], ident[:])
                signals_filled(mm, *g)

            def tok(i):
                return slice(i * P, (i + 1) * P)

            def half(h):
                return slice(h * 512, (h + 1) * 512)

            pe.wait_ge(wq1_in, 32)
            for c in range(DC):
                product(("m1", c), 512, [(wq1T[:, e, tok(c)], wk1T[:, e, :]) for e in range(DC)])
            pe.wait_ge(consts_in, 16 * 16)
            for i in range(NT):
                pe.wait_ge(ln_norm, i + 1)
                transpose_rows(("t0", i), hr[:, i, :])
            for c in range(DC):
                wait_evacuated(pe, "m1", c)
            for h in range(2):
                for i in range(4 * h, 4 * h + 4):
                    wait_evacuated(pe, "t0", i)
                for c in range(DC):
                    product(("gt", c, h), 512, [(m1[:, d, tok(c)], hT[:, d, half(h)]) for d in range(DC)])
            for h in range(2):
                for c in range(DC):
                    wait_evacuated(pe, "gt", c, h)
                wait_bank_free(pe, "e", h)
                for q in range(4):
                    for d in range(DC):
                        mm = nc.tensor.matmul(bank("e", h)[:, q * P:(q + 1) * P], gT[:, d, tok(4 * h + q)],
                                              hT[:, d, tok(4 * h + q)], start=(d == 0), stop=(d == DC - 1))
                signals_filled(mm, "e", h)
            pe.wait_ge(wv1_in, 16)
            for i in range(NT):
                product(("v", i), 512, [(hT[:, d, tok(i)], wv1[:, d, :]) for d in range(DC)])
            for h in range(2):
                pe.wait_ge(sa_cnt, h + 1)
                product(("len", h), 4, [(sel[:], cnt[:, 4 * h:4 * h + 4])])
            pe.wait_ge(wq2_in, 32)
            for c in range(DC):
                product(("m2", c), 512, [(wq2T[:, e, tok(c)], wk2T[:, e, :]) for e in range(DC)])
            for i in range(NT):
                pe.wait_ge(sa_prob, i // 4 + 1)
                wait_bank_free(pe, "pt", i)
                signals_filled(nc.tensor.transpose(bank("pt", i)[:, 0:P], sP[:, i, :], ident[:]), "pt", i)
            for i in range(NT):
                wait_evacuated(pe, "pt", i)
                wait_evacuated(pe, "v", i)
                product(("z", i), 512, [(sT[:, i, :], vv[:, i, :])])
            for i in range(NT):
                pe.wait_ge(ln_out, i + 1)
                transpose_rows(("t1", i), hr[:, i, :])
            for c in range(DC):
                wait_evacuated(pe, "m2", c)
            for h in range(2):
                for i in range(4 * h, 4 * h + 4):
                    wait_evacuated(pe, "t1", i)
                for c in range(DC):
                    product(("q", c, h), 512, [(m2[:, d, tok(c)], hT[:, d, half(h)]) for d in range(DC)])
            for h in range(2):
                for c in range(DC):
                    wait_evacuated(pe, "q", c, h)

            def transpose_block(n, landed, j, kb, first=False):
                pe.wait_ge(ctx_in[j][kb], landed)
                if kb == KB:
                    pe.wait_ge(tp_low, n * 13 + 9)
                    for d in range(DC):
                        mm = nc.tensor.transpose(ps[:, 0, d * TAIL:(d + 1) * TAIL],
                                                 cbuf[j][0:TAIL, KT, d * P:(d + 1) * P], ident[0:TAIL, 0:TAIL])
                    mm.then_inc(tp_done, 1)
                    return
                for d in range(DC):
                    if kb:
                        pe.wait_ge(tp_low, n * 13 + (4 * kb - 3 + d))
                    elif d == 0 and not first:
                        pe.wait_ge(tp_low, n * 13)
                    for t in range(4):
                        mm = nc.tensor.transpose(ps[:, d, t * P:(t + 1) * P],
                                                 cbuf[j][:, 4 * kb + t, d * P:(d + 1) * P], ident[:])
                    mm.then_inc(tp_done, 1)

            def scores(n, j, kb, first=False):
                if kb == 0:
                    pe.wait_ge(q_ready, n + 1)
                pe.wait_ge(tp_low, n * 13 + min(4 * kb + 4, 13))
                if not (first and kb < 2):
                    pe.wait_ge(e_evac, n * 4 + (kb - 1))
                w = TAIL + 1 if kb == KB else 512
                for d in range(DC):
                    for part in range(2):
                        mm = nc.tensor.matmul(ps[:, 4 + kb % 2, 0:w], qs[j][:, d, :], cT[kb % 2][part][:, d, 0:w],
                                              start=(d == 0 and part == 0), stop=(d == DC - 1 and part == 1))
                mm.then_inc(e_done, 1)

            def spread_length(n, j):
                pe.wait_ge(cnt_done, n + 1)
                nc.tensor.matmul(ps[0:S, 6, 256:257], ones[0:1, 0:S], s_cnt[0:1, j, 0:1],
                                 start=True, stop=True).then_inc(len_done, 1)

            def transpose_probabilities(b, j):
                pe.wait_ge(sm_step, b * 9 + 9)
                for t in range(KT + 1):
                    if t == 8:
                        mm.then_inc(pt_done, 1)
                        pe.wait_ge(pt_evac, b * 3 + 1)
                    m = P if t < KT else TAIL
                    dst, src = ps[0:m, 6, (t % 8) * S:(t % 8 + 1) * S], es[j][0:S, t * P:t * P + m]
                    if t % 8 == 0:
                        mm = nc.tensor.matmul(dst, src, ident[0:S, 0:S], start=True, stop=True)
                    else:
                        mm = nc.tensor.transpose(dst, src, ident[0:S, 0:S])
                mm.then_inc(pt_done, 1)

            def values(b, j, n, jn):
                for t in range(KT + 1):
                    if t == 8:
                        pe.wait_ge(pt_evac, b * 3 + 3)
                        if n is not None:
                            spread_length(n, jn)
                    m = P if t < KT else TAIL
                    mm = nc.tensor.matmul(ps[0:S, 7, :], pts[0:m, t, :], cbuf[j][0:m, t, :],
                                          start=(t == 0), stop=(t == KT))
                    if t % 4 == 3 or t == KT:
                        mm.then_inc(pv_done, 1)

            def transpose_output(b, following=True):
                pe.wait_ge(o_copied, b + 1)
                if following:
                    pe.wait_ge(sm_step, b * 9 + (9 + 1))
                for d in range(DC):
                    dst, src = ps[:, 6, d * S:(d + 1) * S], osb[0:S, d * P:(d + 1) * P]
                    if d == 0:
                        mm = nc.tensor.matmul(dst, src, ident[0:S, 0:S], start=True, stop=True)
                    else:
                        mm = nc.tensor.transpose(dst, src, ident[0:S, 0:S])
                mm.then_inc(o_done, 1)

            def step(n, landed, b, jn, jb, first=False):
                transpose_block(n, landed, jn, 0, first)
                for kb in range(1, KB + 1):
                    transpose_block(n, landed, jn, kb, first)
                    scores(n, jn, kb - 1, first)
                    if kb == 1 and not first and not (isinstance(n, int) and n == 1):
                        transpose_output(n - 2)
                scores(n, jn, KB, first)
                if first:
                    spread_length(n, jn)
                    return
                if not (isinstance(n, int) and n == 1):
                    pe.wait_ge(o_evac, n - 1)
                transpose_probabilities(b, jb)
                values(b, jb, n, jn)

            step(0, 16, None, 0, None, first=True)
            step(1, 16, 0, 1, 0)
            with pe.Fori(0, B // CB - 1) as i:
                step(i * CB + 2, i * 16 + 32, i * CB + 1, 0, 1)
                step(i * CB + 3, i * 16 + 32, i * CB + 2, 1, 0)
            transpose_output(B - 2)
            pe.wait_ge(o_evac, B - 1)
            transpose_probabilities(B - 1, 1)
            values(B - 1, 1, None, None)
            transpose_output(B - 1, following=False)

            pe.wait_ge(wv2_in, 16)
            pe.wait_ge(o_evac, B)
            for i in range(NT):
                product(("z2", i), 512, [(qT[:, d, tok(i)], wv2[:, d, :]) for d in range(DC)])
            for i in range(NT):
                pe.wait_ge(ln_out, NT + i + 1)
                transpose_rows(("t2", i), hr[:, i, :])
            pe.wait_ge(fc_in, 32)
            for h in range(2):
                for i in range(4 * h, 4 * h + 4):
                    wait_evacuated(pe, "t2", i)
                for c in range(DC):
                    product(("f1", c, h), 512, [(fc1[:, d, tok(c)], hT[:, d, half(h)]) for d in range(DC)])
            for i in range(NT):
                for c in range(DC):
                    wait_evacuated(pe, "f1", c, i // 4)
                product(("f2", i), 512, [(f1T[:, d, tok(i)], fc2[:, d, :]) for d in range(DC)])
            for i in range(NT):
                pe.wait_ge(ln_norm, 4 * NT + i + 1)
                transpose_rows(("t4", i), hr[:, i, :])
            pe.wait_ge(win_in, 16)
            for i in range(NT):
                wait_evacuated(pe, "t4", i)
            for name, base in (("xh", HC), ("ga", 0)):
                for c in range(HC):
                    for h in range(2):
                        product((name, c, h), 512,
                                [(win[:, d, tok(base + c)], hT[:, d, half(h)]) for d in range(DC)])
            pe.wait_ge(wga_in, 16)
            pe.wait_ge(conv_done, HC)
            for c in range(HC):
                for h in range(2):
                    product(("fg", c, h), 512, [(wga[:, k, tok(c)], xhc[:, k, half(h)]) for k in range(HC)])
            for h in range(2):
                for c in range(HC):
                    product(("ig", c, h), 512, [(wga[:, k, tok(HC + c)], xhc[:, k, half(h)]) for k in range(HC)])
            pe.wait_ge(wout_in, 16)
            for i in range(NT):
                pe.wait_ge(gated, HC * (i // 4 + 1))
                product(("wo", i), 512, [(gel[:, k, tok(i)], wout[:, k, :]) for k in range(HC)])
            for i in range(NT):
                pe.wait_ge(ln_norm, 5 * NT + i + 1)
                transpose_rows(("t5", i), hr[:, i, :])
            wait_bank_free(pe, "lg")
            for i in range(NT):
                wait_evacuated(pe, "t5", i)
                for d in range(DC):
                    mm = nc.tensor.matmul(bank("lg")[:, i * NE:(i + 1) * NE], hT[:, d, tok(i)], gwT[:, d, :],
                                          start=(d == 0), stop=(d == DC - 1))
            signals_filled(mm, "lg")
            pe.wait_ge(oh_done, 1)
            wait_bank_free(pe, "rk")
            W = TOPK * NE
            for i in range(NT):
                for k in range(i + 1):
                    mm = nc.tensor.matmul(bank("rk")[:, i * W:(i + 1) * W], (tri if k == i else ones)[:],
                                          oh[:, TOPK * k:TOPK * k + TOPK, :].rearrange("p k e -> p (k e)"),
                                          start=(k == 0), stop=(k == i))
            signals_filled(mm, "rk")

            def slots(s):
                return P if s < NS - 1 else LAST

            def transpose_slots(n, j, s, first=False):
                if s == 0:
                    pe.wait_ge(xe_in[j], n["half"] * 32 + 32)
                if not (first and s == 0):
                    pe.wait_ge(xt_low, n["n"] * NS + s)
                m = slots(s)
                for d in range(DC):
                    dst, src = ps[:, 7, d * m:(d + 1) * m], xe[j][0:m, s, d * P:(d + 1) * P]
                    if d == 0 and m == LAST:
                        mm = nc.tensor.matmul(dst, src, ident[0:m, 0:m], start=True, stop=True)
                    else:
                        mm = nc.tensor.transpose(dst, src, ident[0:m, 0:m])
                mm.then_inc(xt_done, 1)

            def gate_up(n, j, f, first=False):
                pe.wait_ge(w_low, n["n"] * FC + (f + 1))
                if f == 0:
                    pe.wait_ge(xt_low, n["n"] * NS + NS)
                if not (first and f < 2):
                    pe.wait_ge(hid_done, n["n"] * FC + (f - 1))
                for part in range(2):
                    for d in range(DC):
                        c = (part * DC + d) * P
                        for w, x in ((0, 0), (0, 1), (1, 0)):
                            mm = nc.tensor.matmul(ps[:, 2 * part + f % 2, 0:SLOTS], wsplit[f % RING][w][:, c:c + P],
                                                  xsplit[j][x][:, d, :], start=(d == 0 and w + x == 0),
                                                  stop=(d == DC - 1 and w == 1))
                    mm.then_inc(gu_done, 1)

            def down(n, f, first=False):
                pe.wait_ge(hid_low, n["n"] * (2 * FC) + (2 * f + 2))
                h, wh, wl = hsplit[f % 2], wsplit[f % RING][0][:, 2 * DC * P:UW], wsplit[f % RING][1][:, 2 * DC * P:UW]
                for s in range(NS):
                    if f == 0 and not first:
                        pe.wait_ge(y_evac, n["n"] * NS + (s - NS + 1))
                    hi = h[:, s * P:(s + 1) * P]
                    low = SLOTS + LAST + s * P
                    terms = [(hi, wh), (hi, wl)] + ([(h[:, low:low + P], wh)] if s < NS - 1 else [])
                    for k, (x, w) in enumerate(terms):
                        mm = nc.tensor.matmul(ps[:, 4 + s, :], x, w, start=(f == 0 and k == 0),
                                              stop=(f == FC - 1 and k == len(terms) - 1))
                mm.then_inc(down_done, 1)

            def expert(n, j, nxt, first=False, last=False):
                for f in range(FC):
                    if f < FC - 1:
                        gate_up(n, j, f + 1, first)
                    elif not last:
                        gate_up(nxt, 1 - j, 0)
                    down(n, f, first)
                    if f in (1, 3, 4) and not last:
                        transpose_slots(nxt, 1 - j, (f - 1 + 1) // 2)

            def nth(n, half):
                return {"n": n, "half": half}

            wait_evacuated(pe, "rk")
            for s in range(NS):
                transpose_slots(nth(0, 0), 0, s, first=True)
            gate_up(nth(0, 0), 0, 0, first=True)
            expert(nth(0, 0), 0, nth(1, 0), first=True)
            with pe.Fori(0, NE // 2 - 1) as i:
                expert(nth(i * 2 + 1, i), 1, nth(i * 2 + 2, i + 1))
                expert(nth(i * 2 + 2, i + 1), 0, nth(i * 2 + 3, i + 1))
            expert(nth(NE - 1, NE // 2 - 1), 1, None, last=True)

        @block.scalar
        def _(act):
            def copy_out(dst, src_bank, g):
                wait_filled(act, *g)
                signals_evacuated(nc.scalar.copy(dst, src_bank), *g)

            def transposed_out(name, i):
                copy_out(hT[:, :, i * P:(i + 1) * P], bank(name, i).rearrange("p (c t) -> p c t", t=P), (name, i))

            for c in range(DC):
                copy_out(m1[:, c, :], bank("m1", c), ("m1", c))
            for i in range(NT):
                transposed_out("t0", i)
            for h in range(2):
                for c in range(DC):
                    copy_out(gT[:, c, h * 512:(h + 1) * 512], bank("gt", c, h), ("gt", c, h))
            for i in range(NT):
                copy_out(vv[:, i, :], bank("v", i), ("v", i))
            for c in range(2):
                copy_out(m2[:, c, :], bank("m2", c), ("m2", c))
            for h in range(2):
                act.wait_ge(sa_shift, h + 1)
                hs = slice(4 * h, 4 * h + 4)
                nc.scalar.activation(sP[:, hs, :], sP[:, hs, :], ACT.Exp, scale=SCALE).then_inc(sa_exp, 1)
            for c in range(2, DC):
                copy_out(m2[:, c, :], bank("m2", c), ("m2", c))
            for i in range(NT):
                copy_out(sT[:, i, :], bank("pt", i)[:, 0:P], ("pt", i))
            for i in range(NT):
                transposed_out("t1", i)
            for h in range(2):
                for c in range(DC):
                    copy_out(qT[:, c, h * 512:(h + 1) * 512], bank("q", c, h), ("q", c, h))

            def block_out(n, kb, first=False):
                if not (first and kb < 2):
                    act.wait_ge(e_done, n * 4 + (kb - 1))
                if kb == KB:
                    act.wait_ge(tp_done, n * 13 + 13)
                    nc.scalar.copy(cT[kb % 2][0][:, :, 0:TAIL],
                                   ps[:, 0, 0:DC * TAIL].rearrange("p (c t) -> p c t", t=TAIL)).then_inc(tp_high, 1)
                    return
                for d in range(DC):
                    act.wait_ge(tp_done, n * 13 + (4 * kb + d + 1))
                    nc.scalar.copy(cT[kb % 2][0][:, d, :], ps[:, d, :]).then_inc(tp_high, 1)

            def scores_high(n, j, kb):
                act.wait_ge(e_done, n * 4 + (kb + 1))
                w = TAIL if kb == KB else 512
                nc.scalar.copy(es[j][0:S, kb * 512:kb * 512 + w], ps[S:P, 4 + kb % 2, 0:w]).then_inc(e_high, 1)

            def probabilities(b, j):
                act.wait_ge(sm_step, b * 9 + 6)
                nc.scalar.activation(es[j][0:S, :], es[j][0:S, :], ACT.Exp, bias=s_cnt[:, j, 5:6], scale=SCALE,
                                     accum_out=s_cnt[:, j, 6:7]).then_inc(exp_done, 1)

            def output_copy(b):
                act.wait_ge(pv_done, b * (KB + 1) + (KB + 1))
                nc.scalar.copy(osb[0:S, :], ps[0:S, 7, :]).then_inc(o_copied, 1)

            def step(n, b, j, first=False):
                block_out(n, 0, first)
                block_out(n, 1, first)
                scores_high(n, j, 0)
                block_out(n, 2)
                scores_high(n, j, 1)
                block_out(n, KB)
                scores_high(n, j, 2)
                scores_high(n, j, 3)
                probabilities(n, j)
                if not first:
                    output_copy(b)

            step(0, None, 0, first=True)
            step(1, 0, 1)
            with act.Fori(0, B // CB - 1) as i:
                step(i * CB + 2, i * CB + 1, 0)
                step(i * CB + 3, i * CB + 2, 1)
            output_copy(B - 1)

            for i in range(NT):
                transposed_out("t2", i)
            for h in range(2):
                for c in range(DC):
                    wait_filled(act, "f1", c, h)
                    signals_evacuated(nc.scalar.activation(f1T[:, c, h * 512:(h + 1) * 512], bank("f1", c, h),
                                                           ACT.Relu, bias=fc1b[:, c:c + 1]), "f1", c, h)
            act.wait_ge(lac_step, 2)
            nc.scalar.activation(lac[:, 1, :], lac[:, 0, :], ACT.Exp).then_inc(lac_done, 1)
            for i in range(NT):
                transposed_out("t4", i)
            for c in range(HC):
                if c >= 2:
                    act.wait_ge(conv_done, c - 1)
                for h in range(2):
                    copy_out(raw[c % 2][:, h * 512:(h + 1) * 512], bank("xh", c, h), ("xh", c, h))
            for c in range(HC):
                for h in range(2):
                    wait_filled(act, "ga", c, h)
                    signals_evacuated(nc.scalar.activation(gel[:, c, h * 512:(h + 1) * 512], bank("ga", c, h),
                                                           ACT.Gelu), "ga", c, h)
            for c in range(HC):
                for h in range(2):
                    wait_filled(act, "fg", c, h)
                    signals_evacuated(nc.scalar.activation(alp[:, c, h * 512:(h + 1) * 512], bank("fg", c, h),
                                                           ACT.Sigmoid, bias=bgate[:, c:c + 1]), "fg", c, h)
            act.wait_ge(lac_step, LAC_STEPS)
            for c in range(HC):
                for h in range(2):
                    wait_evacuated(act, "fg", c, h)
                nc.scalar.activation(alp[:, c, :], alp[:, c, :], ACT.Exp, scale=lac[:, 7, c:c + 1]).then_inc(alpha_done, 1)
            for c in range(HC):
                act.wait_ge(square_done, c + 1)
                nc.scalar.activation(bet[c], bet[c], ACT.Sqrt, bias=consts[:, 1:2], scale=-1.0).then_inc(beta_done, 1)
            for h in range(2):
                for c in range(HC):
                    k = h * HC + c
                    if k >= 2:
                        act.wait_ge(rec_step, 3 * (k - 2) + 1)
                    wait_filled(act, "ig", c, h)
                    signals_evacuated(nc.scalar.activation(sgi[k % 2], bank("ig", c, h), ACT.Sigmoid,
                                                           bias=bgate[:, HC + c:HC + c + 1]), "ig", c, h)
            for i in range(NT):
                transposed_out("t5", i)
            act.wait_ge(rt_shift, 1)
            nc.scalar.activation(lg[:], lg[:], ACT.Exp).then_inc(rt_exp, 1)

            def split_high(n, f, first=False):
                act.wait_ge(w_in[f % RING], n * (16 * FC // RING) + (16 * (f // RING) + 16))
                if not first:
                    act.wait_ge(down_done, n * FC + (f - RING + 1))
                nc.scalar.copy(wsplit[f % RING][0][:], wraw[f % RING]).then_inc(w_high, 1)

            def slots_out(n, j, s):
                m = P if s < NS - 1 else LAST
                act.wait_ge(xt_done, n * NS + (s + 1))
                nc.scalar.copy(xsplit[j][0][:, :, s * P:s * P + m],
                               ps[:, 7, 0:DC * m].rearrange("p (c m) -> p c m", m=m)).then_inc(xt_high, 1)

            def tail_out(n, first=False):
                act.wait_ge(down_done, n * FC + FC)
                if not first:
                    act.wait_ge(y_evac, n * NS)
                nc.scalar.copy(ytail[0:LAST, :], ps[LAST:P, 4 + NS - 1, :]).then_inc(tail_high, 1)

            def expert(n, j, first=False, last=False, second=False):
                for f in range(FC):
                    act.wait_ge(gu_done, n * (2 * FC) + (2 * f + 1))
                    if not (first and f < 2):
                        act.wait_ge(hid_done, n * FC + (f - 1))
                    nc.scalar.activation(sg[f % 2], ps[:, f % 2, 0:SLOTS], ACT.Silu).then_inc(silu_done, 1)
                    act.wait_ge(hid_done, n * FC + (f + 1))
                    if not (first and f < 2):
                        act.wait_ge(down_done, n * FC + (f - 1))
                    nc.scalar.copy(hsplit[f % 2][:, 0:SLOTS], hid[f % 2]).then_inc(hid_high, 1)
                    if f == 0 and not first:
                        tail_out(n - 1, second)
                    if not (last and f + AHEAD >= FC):
                        split_high(n + (f + AHEAD) // FC, (f + AHEAD) % FC, first and f + AHEAD < RING)
                    if f in (2, 4, 5) and not last:
                        slots_out(n + 1, 1 - j, (f - 1) // 2 if f < 5 else 2)

            for i in range(NT):
                wait_filled(act, "wo", i)
            for f in range(AHEAD):
                split_high(0, f, first=True)
            for s in range(NS):
                slots_out(0, 0, s)
            expert(0, 0, first=True)
            expert(1, 1, second=True)
            expert(2, 0)
            with act.Fori(0, NE // 2 - 2) as i:
                expert(i * 2 + 3, 1)
                expert(i * 2 + 4, 0)
            expert(NE - 1, 1, last=True)
            tail_out(NE - 1)

        @block.vector
        def _(dve):
            V = nc.vector

            def norm_stats(L, i, src):
                n = L * NT + i + 1
                V.bn_stats(stats[:, i, :], src).then_inc(ln_stats, 1)
                dve.wait_ge(ln_stats, n)
                V.bn_aggr(mv[:, i, :], stats[:, i, :]).then_inc(ln_mv, 1)

            def norm_apply(L, i, src):
                dve.wait_ge(ln_rstd, L * NT + i + 1)
                V.tensor_scalar(hr[:, i, :], src, mv[:, i, 0:1], rstd[:, i:i + 1],
                                ALU.subtract, ALU.mult).then_inc(ln_norm, 1)

            def bc(col):
                return col.unsqueeze(2).to_broadcast([P, 4, P])

            def mask4(m):
                return m[:].unsqueeze(1).to_broadcast([P, 4, P])

            for i in range(NT):
                if i % 2 == 0:
                    dve.wait_ge(x_in[i // 2], 16)
                norm_stats(0, i, xr[:, i, :])
                if i:
                    norm_apply(0, i - 1, xr[:, i - 1, :])
            norm_apply(0, NT - 1, xr[:, NT - 1, :])

            dve.wait_ge(consts_in, 16 * 16)
            steps = [0]

            def chained(ins):
                steps[0] += 1
                ins.then_inc(sa_step, 1)
                dve.wait_ge(sa_step, steps[0])

            hs = [slice(0, 4), slice(4, 8)]
            for h in range(2):
                e4 = bank("e", h).rearrange("p (q k) -> p q k", k=P)
                wait_filled(dve, "e", h)
                chained(V.scalar_tensor_tensor(ne[:, hs[h], :], e4, 0.0, mask4(own), ALU.not_equal, ALU.mult))
                signals_evacuated(V.tensor_tensor(sP[:, hs[h], :], e4, mask4(cmask), ALU.add), "e", h)
                V.tensor_reduce(cnt[:, hs[h]], ne[:, hs[h], :], AX_X, ALU.add).then_inc(sa_cnt, 1)
            for h in range(2):
                wait_filled(dve, "len", h)
                signals_evacuated(V.tensor_copy(lens[:, hs[h]], bank("len", h)[:, 0:4]), "len", h)
                wait_evacuated(dve, "len", h)
                chained(V.reciprocal(rlen[:, hs[h]], lens[:, hs[h]]))
                V.tensor_tensor(onel[:, hs[h]], rlen[:, hs[h]], lens[:, hs[h]], ALU.mult).then_inc(sa_step, 1)
                steps[0] += 1
                chained(V.tensor_tensor(pad[:, hs[h], :], mask4(kidx_self), bc(lens[:, hs[h]]), ALU.is_ge))
                chained(V.scalar_tensor_tensor(sP[:, hs[h], :], pad[:, hs[h], :], NEG, sP[:, hs[h], :],
                                               ALU.mult, ALU.add))
                chained(V.tensor_reduce(mx[:, hs[h]], sP[:, hs[h], :], AX_X, ALU.max))
                V.tensor_tensor(sP[:, hs[h], :], sP[:, hs[h], :], bc(mx[:, hs[h]]), ALU.subtract).then_inc(sa_shift, 1)
            for h in range(2):
                dve.wait_ge(sa_exp, h + 1)
                chained(V.tensor_reduce(rsum[:, hs[h]], sP[:, hs[h], :], AX_X, ALU.add))
                chained(V.reciprocal(rinv[:, hs[h]], rsum[:, hs[h]]))
                chained(V.tensor_tensor(rinv[:, hs[h]], rinv[:, hs[h]], onel[:, hs[h]], ALU.mult))
                V.tensor_tensor(sP[:, hs[h], :], sP[:, hs[h], :], bc(rinv[:, hs[h]]), ALU.mult).then_inc(sa_prob, 1)

            added = [0]

            def residual(name, i, into):
                wait_filled(dve, name, i)
                ins = V.tensor_tensor(into, into, bank(name, i), ALU.add)
                signals_evacuated(ins, name, i)
                wait_evacuated(dve, name, i)

            for i in range(NT):
                residual("z", i, hr[:, i, :])
                norm_stats(1, i, hr[:, i, :])
                if i:
                    norm_apply(1, i - 1, hr[:, i - 1, :])
            norm_apply(1, NT - 1, hr[:, NT - 1, :])

            dve.wait_ge(xs_zeroed, 16)

            def block_out(n, kb):
                if kb == KB:
                    dve.wait_ge(tp_high, n * 13 + 13)
                    V.tensor_tensor(cT[kb % 2][1][:, :, 0:TAIL],
                                    ps[:, 0, 0:DC * TAIL].rearrange("p (c t) -> p c t", t=TAIL),
                                    cT[kb % 2][0][:, :, 0:TAIL].bitcast(F32), ALU.subtract).then_inc(tp_low, 1)
                    return
                for d in range(DC):
                    dve.wait_ge(tp_high, n * 13 + (4 * kb + d + 1))
                    V.tensor_tensor(cT[kb % 2][1][:, d, :], ps[:, d, :], cT[kb % 2][0][:, d, :].bitcast(F32),
                                    ALU.subtract).then_inc(tp_low, 1)

            def scores_out(n, j, kb):
                dve.wait_ge(e_high, n * 4 + (kb + 1))
                w = TAIL if kb == KB else 512
                cols = slice(kb * 512, kb * 512 + w)
                V.tensor_tensor(es[j][0:S, cols], es[j][0:S, cols], ps[0:S, 4 + kb % 2, 0:w], ALU.add)\
                    .then_inc(e_evac, 1)

            def count_keys(n, j):
                dve.wait_ge(e_evac, n * 4 + 4)
                V.tensor_scalar(kpad[0:1, :], es[j][0:1, :], 0.0, None, ALU.not_equal,
                                ALU.add, accum_out=s_cnt[0:1, j, 0:1]).then_inc(cnt_done, 1)

            def shift(b, j):
                c = s_cnt
                dve.wait_ge(len_done, b + 1)
                V.tensor_copy(c[:, j, 1:2], ps[0:S, 6, 256:257]).then_inc(sm_step, 1)
                dve.wait_ge(sm_step, b * 9 + 1)
                V.reciprocal(c[:, j, 2:3], c[:, j, 1:2]).then_inc(sm_step, 1)
                V.tensor_scalar(kpad[0:S, :], kidx[0:S, 0:SK], c[:, j, 1:2], NEG, ALU.is_ge, ALU.mult).then_inc(sm_step, 1)
                dve.wait_ge(sm_step, b * 9 + 3)
                V.tensor_tensor(c[:, j, 3:4], c[:, j, 1:2], c[:, j, 2:3], ALU.mult).then_inc(sm_step, 1)

            def shift_max(b, j):
                c = s_cnt
                V.tensor_tensor_reduce(es[j][0:S, :], es[j][0:S, :], kpad[0:S, :], 1.0, -3e38, ALU.add, ALU.max,
                                       c[:, j, 4:5]).then_inc(sm_step, 1)
                dve.wait_ge(sm_step, b * 9 + 5)
                V.tensor_scalar(c[:, j, 5:6], c[:, j, 4:5], -SCALE, None, ALU.mult).then_inc(sm_step, 1)

            def normalise(b, j):
                c = s_cnt
                dve.wait_ge(exp_done, b + 1)
                V.reciprocal(c[:, j, 7:8], c[:, j, 6:7]).then_inc(sm_step, 1)
                dve.wait_ge(sm_step, b * 9 + 7)
                V.tensor_tensor(c[:, j, 7:8], c[:, j, 7:8], c[:, j, 3:4], ALU.mult).then_inc(sm_step, 1)
                dve.wait_ge(sm_step, b * 9 + 8)
                V.tensor_scalar(es[j][0:S, :], es[j][0:S, :], c[:, j, 7:8], None, ALU.mult).then_inc(sm_step, 1)

            def probabilities_out(b, part):
                dve.wait_ge(pt_done, b * 2 + (part + 1))
                if part == 0:
                    V.tensor_copy(pts[:, 0:8, :], ps[:, 6, :].rearrange("p (t q) -> p t q", q=S)).then_inc(pt_evac, 1)
                    return
                V.tensor_copy(pts[:, 8:KT, :], ps[:, 6, 0:(KT - 8) * S].rearrange("p (t q) -> p t q", q=S))\
                    .then_inc(pt_evac, 1)
                V.tensor_copy(pts[0:TAIL, KT, :], ps[0:TAIL, 6, (KT - 8) * S:(KT - 7) * S]).then_inc(pt_evac, 1)

            def output_out(b):
                dve.wait_ge(o_done, b + 1)
                V.tensor_copy(qT[:, :, bass.ds(b * S, S)],
                              ps[:, 6, 0:DC * S].rearrange("p (c q) -> p c q", q=S)).then_inc(o_evac, 1)

            def step(n, b, j, output=True, first=False):
                block_out(n, 0)
                block_out(n, 1)
                scores_out(n, j, 0)
                if output:
                    output_out(n - 2)
                block_out(n, 2)
                scores_out(n, j, 1)
                block_out(n, KB)
                scores_out(n, j, 2)
                scores_out(n, j, 3)
                if first:
                    count_keys(n, j)
                else:
                    probabilities_out(b, 0)
                    count_keys(n, j)
                    probabilities_out(b, 1)
                shift(n, j)
                shift_max(n, j)
                normalise(n, j)

            step(0, None, 0, output=False, first=True)
            step(1, 0, 1, output=False)
            with dve.Fori(0, B // CB - 1) as i:
                step(i * CB + 2, i * CB + 1, 0)
                step(i * CB + 3, i * CB + 2, 1)
            output_out(B - 2)
            probabilities_out(B - 1, 0)
            probabilities_out(B - 1, 1)
            output_out(B - 1)

            dve.wait_ge(lnw_in, 16)
            for i in range(NT):
                residual("z2", i, hr[:, i, :])
                norm_stats(2, i, hr[:, i, :])
                if i:
                    norm_apply(2, i - 1, hr[:, i - 1, :])
            norm_apply(2, NT - 1, hr[:, NT - 1, :])

            lsteps = [0]

            def lac_chained(ins):
                lsteps[0] += 1
                ins.then_inc(lac_step, 1)
                dve.wait_ge(lac_step, lsteps[0])

            lac_chained(V.tensor_scalar(lac[:, 1, :], fbase[:], -1.0, None, ALU.mult))
            lac_chained(V.tensor_tensor(lac[:, 0, :], fbase[:], lac[:, 1, :], ALU.min))
            dve.wait_ge(lac_done, 1)
            lac_chained(V.tensor_scalar(lac[:, 2, :], lac[:, 1, :], 2.0, None, ALU.add))
            lac_chained(V.reciprocal(lac[:, 3, :], lac[:, 2, :]))
            lac_chained(V.tensor_tensor(lac[:, 2, :], lac[:, 1, :], lac[:, 3, :], ALU.mult))
            V.tensor_tensor(lac[:, 3, :], lac[:, 2, :], lac[:, 2, :], ALU.mult).then_inc(lac_step, 1)
            V.memset(lac[:, 4, :], 1.0 / (2 * ATANH_TERMS - 1)).then_inc(lac_step, 1)
            lsteps[0] += 2
            dve.wait_ge(lac_step, lsteps[0])
            for k in range(ATANH_TERMS - 2, 0, -1):
                lac_chained(V.tensor_tensor(lac[:, 4, :], lac[:, 4, :], lac[:, 3, :], ALU.mult))
                lac_chained(V.tensor_scalar(lac[:, 4, :], lac[:, 4, :], 1.0 / (2 * k + 1), None, ALU.add))
            lac_chained(V.tensor_tensor(lac[:, 4, :], lac[:, 4, :], lac[:, 3, :], ALU.mult))
            V.tensor_scalar(lac[:, 5, :], fbase[:], 0.0, -8.0, ALU.max, ALU.mult).then_inc(lac_step, 1)
            lsteps[0] += 1
            lac_chained(V.scalar_tensor_tensor(lac[:, 6, :], lac[:, 4, :], 1.0, lac[:, 2, :], ALU.add, ALU.mult))
            lac_chained(V.scalar_tensor_tensor(lac[:, 7, :], lac[:, 6, :], -16.0, lac[:, 5, :], ALU.mult, ALU.add))
            assert lsteps[0] == LAC_STEPS, lsteps

            halves = [0]
            for i in range(NT):
                residual("f2", i, hr[:, i, :])
                V.tensor_tensor(hr[:, i, :], hr[:, i, :], lnw[:, 6, :], ALU.add).then_inc(res_half, 1)
                dve.wait_ge(res_half, i + 1)
                norm_stats(3, i, hr[:, i, :])
                if i:
                    norm_apply(3, i - 1, hr[:, i - 1, :])
            norm_apply(3, NT - 1, hr[:, NT - 1, :])
            for i in range(NT):
                dve.wait_ge(ln_out, 2 * NT + i + 1)
                V.tensor_tensor(xr[:, i, :], xr[:, i, :], hr[:, i, :], ALU.add).then_inc(res_sum, 1)
                dve.wait_ge(res_sum, i + 1)
                norm_stats(4, i, xr[:, i, :])
                if i:
                    norm_apply(4, i - 1, xr[:, i - 1, :])
            norm_apply(4, NT - 1, xr[:, NT - 1, :])

            for c in range(HC):
                src = raw[c % 2].rearrange("p (b s) -> p b s", s=S)
                dst = xhc[:, c, :].rearrange("p (b s) -> p b s", s=S)
                for h in range(2):
                    wait_evacuated(dve, "xh", c, h)
                V.tensor_scalar(xhc[:, c, :], raw[c % 2], convw[:, c, 3:4], convb[:, c:c + 1],
                                ALU.mult, ALU.add).then_inc(conv_step, 1)
                for k in range(3):
                    back = 3 - k
                    dve.wait_ge(conv_step, 3 * c + k + 1)
                    V.scalar_tensor_tensor(dst[:, :, back:S], src[:, :, 0:S - back], convw[:, c, k:k + 1],
                                           dst[:, :, back:S], ALU.mult, ALU.add)\
                        .then_inc(conv_step if k < 2 else conv_done, 1)
            for c in range(HC):
                dve.wait_ge(alpha_done, c + 1)
                V.tensor_tensor(bet[c], alp[:, c, :], alp[:, c, :], ALU.mult).then_inc(square_done, 1)
                dve.wait_ge(square_done, c + 1)
                V.memset(alp[:, c, :].rearrange("p (b s) -> p b s", s=S)[:, :, 0:1], 0.0).then_inc(alpha_reset, 1)
            for h in range(2):
                for c in range(HC):
                    k = h * HC + c
                    cols = slice(h * 512, (h + 1) * 512)
                    wait_evacuated(dve, "ig", c, h)
                    dve.wait_ge(beta_done, c + 1)
                    V.tensor_tensor(bet[c][:, cols], bet[c][:, cols], sgi[k % 2], ALU.mult).then_inc(rec_step, 1)
                    dve.wait_ge(rec_step, 3 * k + 1)
                    V.tensor_tensor(bet[c][:, cols], bet[c][:, cols], xhc[:, c, cols], ALU.mult).then_inc(rec_step, 1)
                    dve.wait_ge(rec_step, 3 * k + 2)
                    dve.wait_ge(alpha_reset, c + 1)
                    V.tensor_tensor_scan(bet[c][:, cols], alp[:, c, cols], bet[c][:, cols], 0.0,
                                         ALU.mult, ALU.add).then_inc(rec_step, 1)
                    dve.wait_ge(rec_step, 3 * k + 3)
                    V.tensor_tensor(gel[:, c, cols], gel[:, c, cols], bet[c][:, cols], ALU.mult).then_inc(gated, 1)

            for i in range(NT):
                residual("wo", i, xr[:, i, :])
                norm_stats(5, i, xr[:, i, :])
                if i:
                    norm_apply(5, i - 1, xr[:, i - 1, :])
            norm_apply(5, NT - 1, xr[:, NT - 1, :])

            rsteps = [0]

            def rt_chained(ins):
                rsteps[0] += 1
                ins.then_inc(rt_step, 1)
                dve.wait_ge(rt_step, rsteps[0])

            def over_e(col, n=NT):
                return col.unsqueeze(2).to_broadcast([P, n, NE])

            wait_filled(dve, "lg")
            signals_evacuated(V.tensor_copy(lg[:], bank("lg")[:, 0:NT * NE].rearrange("p (i e) -> p i e", e=NE)), "lg")
            wait_evacuated(dve, "lg")
            rt_chained(V.tensor_reduce(mx[:], lg[:], AX_X, ALU.max))
            V.tensor_tensor(lg[:], lg[:], over_e(mx[:]), ALU.subtract).then_inc(rt_shift, 1)
            dve.wait_ge(rt_exp, 1)
            rt_chained(V.tensor_reduce(rsum[:], lg[:], AX_X, ALU.add))
            rt_chained(V.reciprocal(rinv[:], rsum[:]))
            rt_chained(V.tensor_tensor(lg[:], lg[:], over_e(rinv[:]), ALU.mult))
            for i in range(NT):
                rt_chained(V.max(top8[:, i, :], lg[:, i, :]))
                rt_chained(V.max_index(topi[:, i, :], top8[:, i, :], lg[:, i, :]))
            r3 = [rt[:, k, :].rearrange("p (i k) -> p i k", k=TOPK) for k in range(8)]
            rt_chained(V.tensor_copy(r3[0], topi[:, :, 0:TOPK]))
            V.tensor_tensor(oh[:], eidx[:], over_e(rt[:, 0, :], NT * TOPK), ALU.is_equal).then_inc(oh_done, 1)
            dve.wait_ge(oh_done, 1)
            rt_chained(V.tensor_tensor(rsum[:], top8[:, :, 0], top8[:, :, 1], ALU.add))
            rt_chained(V.tensor_scalar(rsum[:], rsum[:], 1e-9, None, ALU.add))
            rt_chained(V.reciprocal(rinv[:], rsum[:]))
            rt_chained(V.tensor_tensor(r3[1], top8[:, :, 0:TOPK], rinv[:].unsqueeze(2).to_broadcast([P, NT, TOPK]),
                                       ALU.mult))
            rt_chained(V.scalar_tensor_tensor(rt[:, 2, :], rt[:, 0, :], float(SLOTS), slot_at[:, 0, :],
                                              ALU.mult, ALU.add))
            wait_filled(dve, "rk")
            signals_evacuated(V.tensor_tensor(
                rk[:], bank("rk")[:, 0:NT * TOPK * NE].rearrange("p (i e) -> p i e", e=NE), oh[:], ALU.mult), "rk")
            wait_evacuated(dve, "rk")
            rt_chained(V.tensor_reduce(rt[:, 3, :], rk[:], AX_X, ALU.add))
            rt_chained(V.tensor_scalar(rt[:, 4, :], rt[:, 3, :], float(CAP), None, ALU.is_le))
            rt_chained(V.tensor_tensor(rt[:, 5, :], rt[:, 3, :], rt[:, 2, :], ALU.add))
            rt_chained(V.tensor_tensor(rt[:, 1, :], rt[:, 1, :], rt[:, 4, :], ALU.mult))
            rt_chained(V.tensor_tensor(rt[:, 6, :], rt[:, 5, :], rt[:, 4, :], ALU.mult))
            rt_chained(V.tensor_tensor(rt[:, 5, :], rt[:, 5, :], slot_at[:, 1, :], ALU.subtract))
            rt_chained(V.tensor_tensor(rt[:, 5, :], rt[:, 5, :], rt[:, 4, :], ALU.mult))
            rt_chained(V.tensor_tensor(rt[:, 5, :], rt[:, 5, :], slot_at[:, 1, :], ALU.add))
            V.tensor_copy(scat[:], rt[:, 5, :]).then_inc(idx_done, 1)
            V.tensor_copy(gath[:], rt[:, 6, :]).then_inc(idx_done, 1)

            def split_low(n, f, first=False):
                dve.wait_ge(w_high, n * FC + (f + 1))
                V.tensor_tensor(wsplit[f % RING][1][:], wraw[f % RING], wsplit[f % RING][0][:].bitcast(F32),
                                ALU.subtract).then_inc(w_low, 1)

            def slots_low(n, j, s):
                m = P if s < NS - 1 else LAST
                dve.wait_ge(xt_high, n * NS + (s + 1))
                V.tensor_tensor(xsplit[j][1][:, :, s * P:s * P + m], ps[:, 7, 0:DC * m].rearrange("p (c m) -> p c m", m=m),
                                xsplit[j][0][:, :, s * P:s * P + m].bitcast(F32), ALU.subtract).then_inc(xt_low, 1)

            def results_out(n, j, half):
                dve.wait_ge(down_done, n * FC + FC)
                if half is not None:
                    dve.wait_ge(y_out[j], half * 32)
                for s in range(NS - 1):
                    V.tensor_copy(ye[j][:, s, :], ps[:, 4 + s, :]).then_inc(y_evac, 1)
                dve.wait_ge(tail_high, n + 1)
                V.tensor_tensor(ye[j][0:LAST, NS - 1, :], ps[0:LAST, 4 + NS - 1, :], ytail[0:LAST, :],
                                ALU.add).then_inc(y_evac, 1)

            def expert(n, j, half=None, first=False, last=False):
                for f in range(FC):
                    dve.wait_ge(gu_done, n * (2 * FC) + (2 * f + 2))
                    dve.wait_ge(silu_done, n * FC + (f + 1))
                    if not (first and f < 2):
                        dve.wait_ge(hid_low, n * (2 * FC) + (2 * f - 2))
                    V.tensor_tensor(hid[f % 2], sg[f % 2], ps[:, 2 + f % 2, 0:SLOTS], ALU.mult).then_inc(hid_done, 1)
                    dve.wait_ge(hid_high, n * FC + (f + 1))
                    h = hsplit[f % 2]
                    for lo, hi, to in ((SLOTS - LAST, SLOTS, SLOTS), (0, SLOTS - LAST, SLOTS + LAST)):
                        V.tensor_tensor(h[:, to:to + hi - lo], hid[f % 2][:, lo:hi], h[:, lo:hi].bitcast(F32),
                                        ALU.subtract).then_inc(hid_low, 1)
                    if f == 0 and not first:
                        results_out(n - 1, 1 - j, half)
                    if not (last and f + AHEAD >= FC):
                        split_low(n + (f + AHEAD) // FC, (f + AHEAD) % FC)
                    if f in (2, 4, 5) and not last:
                        slots_low(n + 1, 1 - j, (f - 1) // 2 if f < 5 else 2)

            for f in range(AHEAD):
                split_low(0, f)
            for s in range(NS):
                slots_low(0, 0, s)
            expert(0, 0, first=True)
            expert(1, 1)
            expert(2, 0)
            with dve.Fori(0, NE // 2 - 2) as i:
                expert(i * 2 + 3, 1, i + 1)
                expert(i * 2 + 4, 0, i + 1)
            expert(NE - 1, 1, NE // 2 - 1, last=True)
            results_out(NE - 1, 1, NE // 2 - 1)

            for i in range(NT):
                dve.wait_ge(yg_in[i % 4], 32 * (i // 4 + 1))
                for k in range(TOPK):
                    V.scalar_tensor_tensor(xr[:, i, :], yg[i % 4][:, k, :], rt[:, 1, TOPK * i + k:TOPK * i + k + 1],
                                           xr[:, i, :], ALU.mult, ALU.add).then_inc(mix_step if k == 0 else out_ready, 1)
                    if k == 0:
                        dve.wait_ge(mix_step, i + 1)

        @block.gpsimd
        def _(pool):
            G = nc.gpsimd
            G.memset(consts[:, 0:1], -0.5).then_inc(consts_set, 1)
            G.memset(consts[:, 1:2], 1.0 + 1e-6).then_inc(consts_set, 1)
            G.memset(zeros, 0.0).then_inc(zero_set, 1)
            pool.wait_ge(zero_set, 1)
            pool.dma_start(xs[0:TRASH, :].rearrange("(r p) d -> p r d", p=P),
                           zeros.unsqueeze(1).to_broadcast([P, TRASH // P, D])).then_inc(xs_zeroed, 16)
            pool.wait_ge(consts_set, 2)

            def norm_scale(L, i):
                n = L * NT + i + 1
                pool.wait_ge(ln_mv, n)
                G.tensor_scalar(veps[:, i:i + 1], mv[:, i, 1:2], EPS, None, ALU.add).then_inc(ln_veps, 1)
                pool.wait_ge(ln_veps, n)
                G.tensor_tensor(rstd[:, i:i + 1], veps[:, i:i + 1], consts[:, 0:1], ALU.pow).then_inc(ln_rstd, 1)

            def gain_and_bias(L, i):
                w = 2 * (L - 1)
                pool.wait_ge(ln_norm, L * NT + i + 1)
                G.tensor_tensor(hr[:, i, :], hr[:, i, :], lnw[:, w, :], ALU.mult).then_inc(ln_gain, 1)
                pool.wait_ge(ln_gain, (L - 1) * NT + i + 1)
                G.tensor_tensor(hr[:, i, :], hr[:, i, :], lnw[:, w + 1, :], ALU.add).then_inc(ln_out, 1)

            def norms(L, gained):
                for i in range(NT):
                    norm_scale(L, i)
                    if gained and i:
                        gain_and_bias(L, i - 1)
                if gained:
                    gain_and_bias(L, NT - 1)

            norms(0, False)
            pool.wait_ge(lnw_in, 16)
            norms(1, True)

            for h in range(2):
                for c in range(DC):
                    wait_evacuated(pool, "q", c, h)

            def queries(n, j):
                G.tensor_copy(qf[j], qT[:, :, bass.ds(n * S, S)]).then_inc(q_high, 1)
                pool.wait_ge(q_high, n * 2 + 1)
                G.tensor_tensor(qs[j][:, :, 0:S], qf[j], ones[:, 0:S].unsqueeze(1).to_broadcast([P, DC, S]),
                                ALU.mult).then_inc(q_high, 1)
                pool.wait_ge(q_high, n * 2 + 2)
                G.tensor_tensor(qs[j][:, :, S:P], qf[j], qs[j][:, :, 0:S].bitcast(F32), ALU.subtract).then_inc(q_ready, 1)

            for j in range(CB):
                queries(j, j)
            with pool.Fori(0, B // CB - 1) as i:
                for j in range(CB):
                    pool.wait_ge(e_done, i * (4 * CB) + (4 * j + 4))
                    queries(i * CB + (CB + j), j)

            norms(2, True)
            norms(3, True)
            norms(4, False)
            norms(5, False)

            pool.wait_ge(idx_done, 2)
            pool.wait_ge(ln_norm, 6 * NT)
            pool.wait_ge(xs_zeroed, 16)
            for i in range(NT):
                for k in range(TOPK):
                    G.indirect_dma_start(xs, bass.IndirectOffsetOnAxis(scat[:, TOPK * i + k:TOPK * i + k + 1], 0),
                                         hr[:, i, :], None).then_inc(scattered, 16)

            def store(n, j):
                pool.wait_ge(y_evac, n * NS + NS)
                rows = ys[bass.ds(n * SLOTS, SLOTS), :]
                pool.dma_start(rows[0:(NS - 1) * P, :].rearrange("(s p) d -> p s d", p=P),
                               ye[j][:, 0:NS - 1, :]).then_inc(y_out[j], 16)
                pool.dma_start(rows[(NS - 1) * P:SLOTS, :], ye[j][0:LAST, NS - 1, :]).then_inc(y_out[j], 16)

            with pool.Fori(0, NE // 2) as i:
                for j in range(2):
                    store(i * 2 + j, j)
            for j in range(2):
                pool.wait_ge(y_out[j], 32 * (NE // 2))
            for i in range(NT):
                if i >= 4:
                    pool.wait_ge(out_ready, i - 3)
                for k in range(TOPK):
                    G.indirect_dma_start(yg[i % 4][:, k, :], None, ys,
                                         bass.IndirectOffsetOnAxis(gath[:, TOPK * i + k:TOPK * i + k + 1], 0))\
                        .then_inc(yg_in[i % 4], 16)


_OUT = "out"


def kernel(**inputs):
    import numpy as np
    import concourse.bacc as bacc
    from concourse.bass_utils import run_bass_kernel_spmd as run

    v = {k: np.asarray(x) for k, x in inputs.items()}
    f = np.float32

    def cols(w, n):
        return np.ascontiguousarray(w.reshape(n, P).T)

    rows, keys = np.arange(P)[:, None], np.arange(P)[None, :]
    same = (rows // S) == (keys // S)
    t_of = (np.arange(NT)[None, :, None] * P + np.arange(P)[:, None, None])
    k_of = np.arange(TOPK)[None, None, :]
    kidx = np.concatenate([(np.arange(P)[None, :] * KT + np.arange(KT)[:, None]).reshape(-1), np.arange(KT * P, SK)])
    arrays = {
        "x": v["x"].reshape(T, D), "ctx": v["ctx_1024"],
        "wq1T": v["L0_xattn_Wq1"].T, "wk1T": v["L0_xattn_Wk1"].T, "wv1": v["L0_xattn_Wv1"],
        "wq2T": v["L0_xattn_Wq2"].T, "wk2T": v["L0_xattn_Wk2"].T, "wv2": v["L0_xattn_Wv2"],
        "fc1_w": v["L0_xattn_fc1_w"], "fc2_w": v["L0_xattn_fc2_w"],
        "lnw": np.stack([v["L0_xattn_" + n] for n in ("ln1_g", "ln1_b", "ln2_g", "ln2_b", "ln3_g", "ln3_b", "fc2_b")]),
        "fc1b": cols(v["L0_xattn_fc1_b"], DC),
        "w_inT": v["L0_attn_W_in"].T, "w_gatesT": v["L0_attn_W_gates"].T, "w_outT": v["L0_attn_W_out"].T,
        "convw": v["L0_attn_conv_w"].reshape(HC, P, 4).transpose(1, 0, 2), "convb": cols(v["L0_attn_conv_b"], HC),
        "bgate": cols(v["L0_attn_b_gates"], 2 * HC), "fbase": cols(v["L0_attn_forget_base"], HC),
        "gwT": v["L0_ffn_gate_w"].T.reshape(DC, P, NE).transpose(1, 0, 2),
        "w_units": np.concatenate(
            [w.reshape(NE, FC, P, DC, P).transpose(0, 1, 4, 3, 2).reshape(NE * FC, P, DC * P)
             for w in (v["L0_ffn_gate_proj_w"], v["L0_ffn_up_proj_w"])]
            + [v["L0_ffn_down_proj_w"].transpose(0, 2, 1).reshape(NE * FC, P, D)], axis=2),
        "ident": np.eye(P, dtype=f), "own": same.astype(f),
        "cmask": np.where(same & (keys <= rows), f(0), f(NEG)), "kidx_self": np.broadcast_to(keys % S, (P, P)).astype(f),
        "sel": (rows == (keys // S) * S).astype(f), "tri": (rows <= keys).astype(f), "ones": np.ones((P, P), f),
        "slot_at": np.stack([np.broadcast_to(CAP * k_of - 1, (P, NT, TOPK)), TRASH + T * k_of + t_of], 1)
        .reshape(P, 2, NT * TOPK).astype(f),
        "eidx": np.broadcast_to(np.arange(NE), (P, NT * TOPK, NE)).astype(f),
        "kidx": np.broadcast_to(kidx, (S, SK)).astype(np.int16),
    }
    arrays = {k: np.ascontiguousarray(x) for k, x in arrays.items()}
    nc = bacc.Bacc("TRN2", target_bir_lowering=False, num_devices=1)
    a = {k: nc.dram_tensor("in_" + k, x.shape, mybir.dt.from_np(x.dtype), kind="ExternalInput").ap() for k, x in arrays.items()}
    out = nc.dram_tensor(_OUT, (T, D), F32, kind="ExternalOutput").ap()
    perceiver_program(nc, a, out)
    r = run(nc, [{"in_" + k: x for k, x in arrays.items()}], core_ids=[0])
    return r.results[0][_OUT].reshape(B, S, D)
```
